# Optimizing a Trainium2 kernel written in Bass

```python
import numpy as np
import jax
import jax.numpy as jnp

def _softmax(x, axis=-1):
    return jax.nn.softmax(x, axis=axis)

def _gelu(x):
    return jax.nn.gelu(x, approximate=True)

def _silu(x):
    return jax.nn.silu(x)

def _sigmoid(x):
    return jax.nn.sigmoid(x)

def _layernorm(x, axis=-1, eps=1e-05):
    m = jnp.mean(x, axis=axis, keepdims=True)
    v = jnp.var(x, axis=axis, keepdims=True)
    return (x - m) / jnp.sqrt(v + eps)

def _scatter_add(tgt, idx, src, axis=0):
    return tgt.at[idx].add(src)

def _segment_sum(src, seg, n):
    return jax.ops.segment_sum(src, seg, n)
kernel_name = 'mk_adj_preln_d2_adj_r2_2014ed'

def setup_inputs(seed: int=0):
    np.random.seed(seed)
    _w = jnp.asarray

    def _rec_inputs():
        import jax
        import jax.numpy as jnp
        _gk = jax.random.key(seed)
        x = -0.000929 + 1 * jax.random.normal(jax.random.fold_in(_gk, 1), (8, 1024, 256), jnp.float32)
        _a = jax.random.bernoulli(jax.random.fold_in(_gk, 2), 0.015625, (1024, 1024))
        adj = _a.astype(jnp.int32)
        return (x, adj)
    x, adj = _rec_inputs()

    def _L0_gnn_setup():
        import jax, jax.numpy as jnp
        import numpy as np
        B, K, DIN, DOUT = (32, 64, 256, 256)
        key = jax.random.key(seed)
        k1, k2, k3, k4 = jax.random.split(key, 4)
        x = jax.random.normal(k1, (B, K, DIN), dtype=jnp.float32)
        adj = jax.random.randint(k2, (K, K), 0, 2, dtype=jnp.int32)
        W = jax.random.normal(k3, (DOUT, 2 * DIN), dtype=jnp.float32) * 0.02
        b = jax.random.normal(k4, (DOUT,), dtype=jnp.float32) * 0.02
        return {'x': x, 'adj': adj, 'W': W, 'b': b}
    _L0_gnn_all = _L0_gnn_setup()
    _L0_gnn_in = {k: v for k, v in _L0_gnn_all.items() if k in ('W', 'b')}
    del _L0_gnn_all

    def _L1_gnn_setup():
        import jax, jax.numpy as jnp
        import numpy as np
        LEAKY_ALPHA = 0.01
        NEG_INF = -1000000000.0
        LN_EPS = 1e-05

        def _gat_heads(x, adj, W, a):
            O = W.shape[-1]
            Wh = jnp.einsum('bnf,hfo->bhno', x, W)
            f1 = jnp.einsum('bhno,ho->bhn', Wh, a[:, :O])
            f2 = jnp.einsum('bhno,ho->bhn', Wh, a[:, O:])
            e = f1[:, :, :, None] + f2[:, :, None, :]
            e = jnp.where(e > 0, e, LEAKY_ALPHA * e)
            e = jnp.where(adj[None, None] > 0, e, NEG_INF)
            attn = jax.nn.softmax(e, axis=-1)
            return jnp.einsum('bhnm,bhmo->bhno', attn, Wh)
        key = jax.random.key(seed)
        ks = jax.random.split(key, 10)
        B, N, F_in, F_hid, H, F_out, D_ff = (8, 1024, 256, 256, 4, 256, 256)
        s = 0.05
        return {'enc_inputs': jax.random.normal(ks[0], (B, N, F_in), jnp.float32), 'adj': jax.random.randint(ks[1], (N, N), 0, 2, jnp.int32), 'W_heads': jax.random.normal(ks[2], (H, F_in, F_hid), jnp.float32) * s, 'a_heads': jax.random.normal(ks[3], (H, 2 * F_hid), jnp.float32) * s, 'W_out': jax.random.normal(ks[4], (H * F_hid, F_out), jnp.float32) * s, 'a_out': jax.random.normal(ks[5], (2 * F_out,), jnp.float32) * s, 'w1': jax.random.normal(ks[6], (F_out, D_ff), jnp.float32) * s, 'b1': jnp.zeros((D_ff,), jnp.float32), 'w2': jax.random.normal(ks[7], (D_ff, F_out), jnp.float32) * s, 'b2': jnp.zeros((F_out,), jnp.float32), 'ln_gamma': jnp.ones((F_out,), jnp.float32), 'ln_beta': jnp.zeros((F_out,), jnp.float32)}
    _L1_gnn_all = _L1_gnn_setup()
    _L1_gnn_in = {k: v for k, v in _L1_gnn_all.items() if k in ('W_heads', 'a_heads', 'W_out', 'a_out', 'w1', 'b1', 'w2', 'b2', 'ln_gamma', 'ln_beta')}
    del _L1_gnn_all
    return {'x': x, 'adj': adj, 'L0_gnn_W': _L0_gnn_in['W'], 'L0_gnn_b': _L0_gnn_in['b'], 'L1_gnn_W_heads': _L1_gnn_in['W_heads'], 'L1_gnn_a_heads': _L1_gnn_in['a_heads'], 'L1_gnn_W_out': _L1_gnn_in['W_out'], 'L1_gnn_a_out': _L1_gnn_in['a_out'], 'L1_gnn_w1': _L1_gnn_in['w1'], 'L1_gnn_b1': _L1_gnn_in['b1'], 'L1_gnn_w2': _L1_gnn_in['w2'], 'L1_gnn_b2': _L1_gnn_in['b2'], 'L1_gnn_ln_gamma': _L1_gnn_in['ln_gamma'], 'L1_gnn_ln_beta': _L1_gnn_in['ln_beta']}

def reference(x, adj, L0_gnn_W, L0_gnn_b, L1_gnn_W_heads, L1_gnn_a_heads, L1_gnn_W_out, L1_gnn_a_out, L1_gnn_w1, L1_gnn_b1, L1_gnn_w2, L1_gnn_b2, L1_gnn_ln_gamma, L1_gnn_ln_beta):
    import jax
    import jax.numpy as jnp

    def _L0_gnn_ref(x, adj, W, b):
        import jax, jax.numpy as jnp
        import numpy as np
        B, K, DIN, DOUT = (32, 64, 256, 256)
        Din = x.shape[-1]
        Wi, Wj = (W[:, :Din], W[:, Din:])
        mi = jnp.einsum('bkd,od->bko', x, Wi)
        mj = jnp.einsum('bkd,od->bko', x, Wj)
        a = adj.astype(x.dtype)
        deg = a.sum(axis=1)
        out = deg[None, :, None] * (mi + b) + jnp.einsum('ij,bjo->bio', a, mj)
        return out

    def _L1_gnn_ref(enc_inputs, adj, W_heads, a_heads, W_out, a_out, w1, b1, w2, b2, ln_gamma, ln_beta):
        import jax, jax.numpy as jnp
        import numpy as np
        LEAKY_ALPHA = 0.01
        NEG_INF = -1000000000.0
        LN_EPS = 1e-05

        def _gat_heads(x, adj, W, a):
            O = W.shape[-1]
            Wh = jnp.einsum('bnf,hfo->bhno', x, W)
            f1 = jnp.einsum('bhno,ho->bhn', Wh, a[:, :O])
            f2 = jnp.einsum('bhno,ho->bhn', Wh, a[:, O:])
            e = f1[:, :, :, None] + f2[:, :, None, :]
            e = jnp.where(e > 0, e, LEAKY_ALPHA * e)
            e = jnp.where(adj[None, None] > 0, e, NEG_INF)
            attn = jax.nn.softmax(e, axis=-1)
            return jnp.einsum('bhnm,bhmo->bhno', attn, Wh)
        B, N, _ = enc_inputs.shape
        h = jax.nn.elu(_gat_heads(enc_inputs, adj, W_heads, a_heads))
        h = jnp.transpose(h, (0, 2, 1, 3)).reshape(B, N, -1)
        out = _gat_heads(h, adj, W_out[None], a_out[None])[:, 0]
        out = jax.nn.elu(out)
        ffn = jnp.maximum(out @ w1 + b1, 0.0) @ w2 + b2
        y = ffn + out
        mu = jnp.mean(y, axis=-1, keepdims=True)
        var = jnp.var(y, axis=-1, keepdims=True)
        return (y - mu) / jnp.sqrt(var + LN_EPS) * ln_gamma + ln_beta
    h = jnp.maximum(_layernorm(x, axis=-1), 0.0)
    x = x + _L0_gnn_ref(h, adj, L0_gnn_W, L0_gnn_b)
    h = jnp.maximum(_layernorm(x, axis=-1), 0.0)
    x = x + _L1_gnn_ref(h, adj, L1_gnn_W_heads, L1_gnn_a_heads, L1_gnn_W_out, L1_gnn_a_out, L1_gnn_w1, L1_gnn_b1, L1_gnn_w2, L1_gnn_b2, L1_gnn_ln_gamma, L1_gnn_ln_beta)
    return x

_drawn_inputs = setup_inputs


def setup_inputs(seed=0):
    import zlib

    import numpy as np

    out = dict(_drawn_inputs(seed))
    spreads = {'L1_gnn_b1': (0.0, 0.39),
     'L1_gnn_b2': (0.0, 0.1),
     'L1_gnn_ln_gamma': (1.0, 0.2),
     'L1_gnn_ln_beta': (0.0, 0.382)}
    factors = {'L1_gnn_a_heads': 8.0, 'L1_gnn_a_out': 8.0}
    for name, (base, spread) in spreads.items():
        noise = np.random.default_rng([zlib.crc32(name.encode()), seed]).standard_normal(out[name].shape)
        drawn = base * np.exp(spread * noise) if base else spread * noise
        out[name] = jnp.asarray(drawn.astype(out[name].dtype))
    for name, factor in factors.items():
        out[name] = (out[name] * factor).astype(out[name].dtype)
    return out
```

```python
from contextlib import ExitStack

import concourse.bass as bass
from concourse import mybir

ALU = mybir.AluOpType
ACT = mybir.ActivationFunctionType
F32, F16, BF16, I32 = mybir.dt.float32, mybir.dt.float16, mybir.dt.bfloat16, mybir.dt.int32
AX = mybir.AxisListType.X

P = 128
LN_EPS = 1e-5
ALPHA = 0.01
UNIT = 2.0 ** -7
LIN = ALPHA / UNIT
STEP = (1.0 - ALPHA) / UNIT
RATIO = (1.0 - ALPHA) / ALPHA
MASKED = -(2.0 ** 100)
LN_LOG = 11
W_LOG = 13
LN_SCALE = 2.0 ** LN_LOG
WH_LOG = 15 - 4
VAL_SCALE = 2.0 ** (WH_LOG - LN_LOG - W_LOG)
VALO_SCALE = 2.0 ** (6 - WH_LOG - W_LOG)
X_SLOTS = 4
PAIR = 2


def build(nc, x, adj, w0, b0, w_heads, a_heads, w_out, a_out, w1, b1, w2, b2, gamma, beta, out):
    B, N, F = x.shape
    H = w_heads.shape[0]
    T = N // P
    KF = F // P
    HF = H * F
    KH = HF // P
    V = F + 2
    NF = 2 * H
    assert H == 4 and T == 8 and KF == 2 and HF == N
    QUADS = {1: T, 2: T // 4}
    UB = 4 * (QUADS[1] + QUADS[2])
    QB = QUADS[1] + QUADS[2]
    DMA = 16

    with ExitStack() as ctx:
        def sb(name, shape, dt, stack=ctx):
            return stack.enter_context(nc.sbuf_tensor(name, shape, dt))

        def sem(name):
            return ctx.enter_context(nc.semaphore(name))

        mask_add = sb("mask_add", [P, T * N], BF16)
        adjT = sb("adjT", [P, T, N], F16)
        diag_deg = sb("diag_deg", [P, T, P], F16)
        deg = sb("deg", [P, T], F32)
        w0T = sb("w0T", [P, 2 * KF, F], F32)
        wh_hi = sb("wh_hi", [P, KF, HF + NF], F16)
        wh_lo = sb("wh_lo", [P, KF, HF + NF], F16)
        wo_hi = sb("wo_hi", [P, KH, V], F16)
        wo_lo = sb("wo_lo", [P, KH, V], F16)
        w1_sb = sb("w1_sb", [P, KF, F], F32)
        w2_sb = sb("w2_sb", [P, KF, F], F32)
        b1_col = sb("b1_col", [P, KF], F32)
        b0_bc = sb("b0_bc", [P, F], F32)
        b2_bc = sb("b2_bc", [P, F], F32)
        gamma_bc = sb("gamma_bc", [P, F], F32)
        beta_bc = sb("beta_bc", [P, F], F32)
        ident = sb("ident", [P, P], F32)
        ident16 = sb("ident16", [P, P], F16)
        ones = sb("ones", [P, P], F32)
        half_neg = sb("half_neg", [P, T], F32)
        sc = sb("sc", [P, 16], F32)
        S_WH, S_WO, S_WA, S_WAO, S_F, S_H, S_HINV, S_OINV, S_FO, S_F1, S_F2, S_FO1, S_FO2 = range(13)

        def scale(i):
            return sc[:, i:i + 1]

        psum = [ctx.enter_context(nc.psum_tensor(f"ps{i}", [P, 1024], F32)) for i in range(4)]
        psA, psB, psC, psD = psum

        with ExitStack() as tmp:
            adj_i = sb("adj_i", [P, T, N], I32, tmp)
            adj16 = sb("adj16", [P, T, N], F16, tmp)
            w0_sb = sb("w0_sb", [P, KF, 2 * F], F32, tmp)
            whf = sb("whf", [P, KF, H, F], F32, tmp)
            wof = sb("wof", [P, KH, F], F32, tmp)
            ah_bc = sb("ah_bc", [P, H, 2, F], F32, tmp)
            ao_bc = sb("ao_bc", [P, 2, F], F32, tmp)
            waf = sb("waf", [P, KF, 2, H], F32, tmp)
            wao = sb("wao", [P, KH, 2], F32, tmp)
            sq = sb("sq", [P, KF * HF], F32, tmp)
            sqo = sb("sqo", [P, KH * F], F32, tmp)
            sqa = sb("sqa", [P, 32], F32, tmp)
            nsq = sb("nsq", [P, 4], F32, tmp)
            ei = sb("ei", [P, 4], I32, tmp)
            ki = sb("ki", [P, 4], I32, tmp)
            kf = sb("kf", [P, 4], F32, tmp)
            ksum = sb("ksum", [P, 2], F32, tmp)
            ebits = sb("ebits", [P, 16], F32, tmp)
            eint = sb("eint", [P, 16], I32, tmp)
            adj_in, w_in, a_in, c_in = sem("adj_in"), sem("w_in"), sem("a_in"), sem("c_in")
            zero_done, ident_done = sem("zero_done"), sem("ident_done")
            adj16_done, sq_done, norm_done = sem("adj16_done"), sem("sq_done"), sem("norm_done")
            at_done, at_copied, w0t_done = sem("at_done"), sem("at_copied"), sem("w0t_done")
            setup_dve = sem("setup_dve")
            with nc.Block() as block:
                @block.sync
                def _(sp):
                    sp.dma_start(adj_i[:, 0:T // 2, :], adj[0:N // 2, :].rearrange("(t p) j -> p t j", p=P)).then_inc(adj_in, DMA)
                    sp.dma_start(adj_i[:, T // 2:T, :], adj[N // 2:N, :].rearrange("(t p) j -> p t j", p=P)).then_inc(adj_in, DMA)
                    sp.dma_start(b0_bc[:, :], b0.partition_broadcast(P)).then_inc(c_in, DMA)
                    sp.dma_start(b2_bc[:, :], b2.partition_broadcast(P)).then_inc(c_in, DMA)
                    sp.dma_start(gamma_bc[:, :], gamma.partition_broadcast(P)).then_inc(c_in, DMA)
                    sp.dma_start(beta_bc[:, :], beta.partition_broadcast(P)).then_inc(c_in, DMA)
                    sp.dma_start(b1_col[:, :], b1.rearrange("(k p) -> p k", p=P), allow_slow_non_contiguous=True).then_inc(c_in, DMA)
                    sp.dma_start(w1_sb[:, :, :], w1.rearrange("(k p) n -> p k n", p=P)).then_inc(c_in, DMA)
                    sp.dma_start(w2_sb[:, :, :], w2.rearrange("(k p) n -> p k n", p=P)).then_inc(c_in, DMA)
                    sp.wait_ge(c_in, 7 * DMA)

                @block.scalar
                def _(act):
                    for k in range(KF):
                        act.dma_start(whf[:, k, :, :], w_heads[:, k * P:(k + 1) * P, :].rearrange("h p f -> p h f")).then_inc(w_in, DMA)
                    act.dma_start(wof[:, :, :], w_out.rearrange("(k p) n -> p k n", p=P)).then_inc(w_in, DMA)
                    act.dma_start(w0_sb[:, :, :], w0.rearrange("(k p) n -> p k n", p=P)).then_inc(w_in, DMA)
                    act.dma_start(ah_bc[:, :, :, :].rearrange("p h c f -> p (h c f)"), a_heads.rearrange("h c -> (h c)").partition_broadcast(P)).then_inc(a_in, DMA)
                    act.dma_start(ao_bc[:, :, :].rearrange("p c f -> p (c f)"), a_out.partition_broadcast(P)).then_inc(a_in, DMA)
                    for jt in range(T):
                        act.wait_ge(at_done, jt + 1)
                        nc.scalar.activation(adjT[:, jt, :], psum[jt % 2][:, 0:N // 2].bitcast(F16), ACT.Copy).then_inc(at_copied, 1)
                    act.wait_ge(w0t_done, 1)
                    nc.scalar.activation(w0T[:, :, :].rearrange("p k n -> p (k n)"), psC[:, :], ACT.Copy).then_inc(at_copied, 1)

                @block.gpsimd
                def _(pool):
                    nc.gpsimd.memset(ident[:, :], 0.0).then_inc(zero_done, 1)
                    nc.gpsimd.memset(ident16[:, :], 0.0).then_inc(zero_done, 1)
                    nc.gpsimd.memset(half_neg[:, :], -0.5)
                    nc.gpsimd.memset(ones[:, :], 1.0)
                    pool.wait_ge(zero_done, 2)
                    for m in (ident, ident16):
                        nc.gpsimd.affine_select(out=m[:, :], in_=m[:, :], compare_op=ALU.not_equal, fill=1.0, base=0,
                                                pattern=[[-1, P]], channel_multiplier=1).then_inc(ident_done, 1)

                @block.vector
                def _(dve):
                    chain = [0]

                    def link(instruction):
                        chain[0] += 1
                        instruction.then_inc(setup_dve, 1)
                        dve.wait_ge(setup_dve, chain[0])

                    for half in range(2):
                        t0 = half * T // 2
                        dve.wait_ge(adj_in, 2 * DMA)
                        nc.vector.tensor_copy(adj16[:, t0:t0 + T // 2, :], adj_i[:, t0:t0 + T // 2, :]).then_inc(adj16_done, 1)
                    dve.wait_ge(adj16_done, 2)
                    nc.vector.tensor_scalar(mask_add[:, :], adj16[:, :, :].rearrange("p t j -> p (t j)"), 0.0, MASKED, ALU.is_le, ALU.mult)
                    link(nc.vector.reduce_sum(deg[:, :], adj16[:, :, :], axis=AX))
                    dve.wait_ge(w_in, 4 * DMA)
                    dve.wait_ge(a_in, 2 * DMA)
                    for c in range(2):
                        for k in range(KF):
                            for h in range(H):
                                link(nc.vector.tensor_tensor_reduce(out=sq[:, 0:F], in0=whf[:, k, h, :], in1=ah_bc[:, h, c, :], scale=1.0, scalar=0.0,
                                                                    op0=ALU.mult, op1=ALU.add, accum_out=waf[:, k, c, h:h + 1]))
                        for k in range(KH):
                            link(nc.vector.tensor_tensor_reduce(out=sq[:, 0:F], in0=wof[:, k, :], in1=ao_bc[:, c, :], scale=1.0, scalar=0.0,
                                                                op0=ALU.mult, op1=ALU.add, accum_out=wao[:, k, c:c + 1]))
                    whf_flat = whf[:, :, :, :].rearrange("p k h f -> p (k h f)")
                    wof_flat = wof[:, :, :].rearrange("p k f -> p (k f)")
                    waf_flat = waf[:, :, :, :].rearrange("p k c h -> p (k c h)")
                    wao_flat = wao[:, :, :].rearrange("p k c -> p (k c)")
                    nc.vector.tensor_tensor(sq[:, :], whf_flat, whf_flat, ALU.mult)
                    nc.vector.tensor_tensor(sqo[:, :], wof_flat, wof_flat, ALU.mult)
                    nc.vector.tensor_tensor(sqa[:, 0:16], waf_flat, waf_flat, ALU.mult)
                    nc.vector.tensor_tensor(sqa[:, 16:32], wao_flat, wao_flat, ALU.mult).then_inc(sq_done, 1)
                    dve.wait_ge(ident_done, 2)
                    for t in range(T):
                        last = nc.vector.tensor_scalar(diag_deg[:, t, :], ident16[:, :], deg[:, t:t + 1], None, ALU.mult)
                    dve.wait_ge(norm_done, 1)
                    nc.vector.reduce_max(nsq[:, 0:1], psA[:, :], axis=AX)
                    nc.vector.reduce_max(nsq[:, 1:2], psB[:, 0:F], axis=AX)
                    nc.vector.reduce_max(nsq[:, 2:3], psD[:, 0:NF], axis=AX)
                    link(nc.vector.reduce_max(nsq[:, 3:4], psD[:, NF:NF + 2], axis=AX))
                    link(nc.vector.tensor_scalar(ei[:, :], nsq[:, :].bitcast(I32), 23, None, ALU.logical_shift_right))
                    link(nc.vector.tensor_scalar(ei[:, :], ei[:, :], 129.0, None, ALU.add))
                    link(nc.vector.tensor_scalar(ki[:, :], ei[:, :], 1, None, ALU.logical_shift_right))
                    link(nc.vector.tensor_copy(kf[:, :], ki[:, :]))
                    nc.vector.tensor_tensor(ksum[:, 0:1], kf[:, 0:1], kf[:, 1:2], ALU.add)
                    link(nc.vector.tensor_tensor(ksum[:, 1:2], kf[:, 0:1], kf[:, 3:4], ALU.add))
                    link(nc.vector.memset(ebits[:, :], 127.0))
                    nc.vector.tensor_scalar(ebits[:, 0:4], kf[:, 0:4], -1.0, 254.0 + W_LOG, ALU.mult, ALU.add)
                    nc.vector.tensor_scalar(ebits[:, S_F:S_F + 1], kf[:, 2:3], -float(LN_LOG + W_LOG), None, ALU.add)
                    nc.vector.tensor_scalar(ebits[:, S_H:S_H + 1], kf[:, 0:1], -1.0, 254.0 + WH_LOG, ALU.mult, ALU.add)
                    nc.vector.tensor_scalar(ebits[:, S_HINV:S_HINV + 1], kf[:, 0:1], -float(WH_LOG), None, ALU.add)
                    nc.vector.tensor_scalar(ebits[:, S_OINV:S_OINV + 1], ksum[:, 0:1], -127.0 - 6.0, None, ALU.add)
                    link(nc.vector.tensor_scalar(ebits[:, S_FO:S_FO + 1], ksum[:, 1:2], -127.0 - float(WH_LOG + W_LOG), None, ALU.add))
                    link(nc.vector.tensor_scalar(eint[:, :], ebits[:, :], 1.0, 254.0, ALU.max, ALU.min))
                    link(nc.vector.tensor_scalar(sc[:, :].bitcast(I32), eint[:, :], 23, None, ALU.logical_shift_left))
                    nc.vector.tensor_scalar(scale(S_F1), scale(S_F), STEP, None, ALU.mult)
                    nc.vector.tensor_scalar(scale(S_F2), scale(S_F), LIN, None, ALU.mult)
                    nc.vector.tensor_scalar(scale(S_FO1), scale(S_FO), STEP, None, ALU.mult)
                    nc.vector.tensor_scalar(scale(S_FO2), scale(S_FO), LIN, None, ALU.mult)
                    for src, hi, lo, s in (
                        (whf[:, :, :, :].rearrange("p k h f -> p k (h f)"), wh_hi[:, :, 0:HF], wh_lo[:, :, 0:HF], S_WH),
                        (waf[:, :, :, :].rearrange("p k c h -> p k (c h)"), wh_hi[:, :, HF:HF + NF], wh_lo[:, :, HF:HF + NF], S_WA),
                        (wof[:, :, :], wo_hi[:, :, 0:F], wo_lo[:, :, 0:F], S_WO),
                        (wao[:, :, :], wo_hi[:, :, F:V], wo_lo[:, :, F:V], S_WAO),
                    ):
                        link(nc.vector.tensor_scalar(hi, src, scale(s), None, ALU.mult))
                        link(nc.vector.scalar_tensor_tensor(lo, src, scale(s), hi, ALU.mult, ALU.subtract))

                @block.tensor
                def _(pe):
                    pe.wait_ge(ident_done, 2)
                    pe.wait_ge(w_in, 4 * DMA)
                    for k in range(2 * KF):
                        for o in range(KF):
                            last = nc.tensor.transpose(psC[:, k * F + o * P:k * F + (o + 1) * P], w0_sb[:, o, k * P:(k + 1) * P], ident[:, :])
                    last.then_inc(w0t_done, 1)
                    pe.wait_ge(adj16_done, 2)
                    for jt in range(T):
                        if jt >= 2:
                            pe.wait_ge(at_copied, jt - 1)
                        for it in range(T):
                            last = nc.tensor.transpose(psum[jt % 2][:, it * P // 2:(it + 1) * P // 2].bitcast(F16),
                                                       adj16[:, it, jt * P:(jt + 1) * P], ident16[:, :])
                        last.then_inc(at_done, 1)
                    pe.wait_ge(at_copied, T)
                    pe.wait_ge(sq_done, 1)
                    for c in range(2):
                        for k in range(KF):
                            nc.tensor.matmul(psA[:, c * 512:(c + 1) * 512], ones[:, :], sq[:, k * HF + c * 512:k * HF + (c + 1) * 512],
                                             start=k == 0, stop=k == KF - 1)
                    for k in range(KH):
                        nc.tensor.matmul(psB[:, 0:F], ones[:, :], sqo[:, k * F:(k + 1) * F], start=k == 0, stop=k == KH - 1)
                    for k in range(KF):
                        nc.tensor.matmul(psD[:, 0:NF], ones[:, :], sqa[:, k * NF:(k + 1) * NF], start=k == 0, stop=k == KF - 1)
                    for k in range(KH):
                        last = nc.tensor.matmul(psD[:, NF:NF + 2], ones[:, :], sqa[:, 16 + 2 * k:18 + 2 * k], start=k == 0, stop=k == KH - 1)
                    last.then_inc(norm_done, 1)

        xx = sb("xx", [P, T, F], F32)
        yy = sb("yy", [P, T, F], F32)
        hs_hi = sb("hs_hi", [P, 2048], F16)
        hs_lo = sb("hs_lo", [P, 2048], F16)
        cat = sb("cat", [P, 4, N], F32)
        val_hi = sb("val_hi", [P, T, H, V], F16)
        val_lo = sb("val_lo", [P, T, H, V], F16)
        valo_hi = sb("valo_hi", [P, T * V], F16)
        valo_lo = sb("valo_lo", [P, T * V], F16)
        f2o = sb("f2o", [P, N], F32)
        f1h = sb("f1h", [P, T * H], F32)
        f1o = sb("f1o", [P, T], F32)
        f2c = sb("f2c", [P, H], F32)
        f2oc = sb("f2oc", [P, 1], F32)
        shift = sb("shift", [P, (T + 2) * 4], F32)
        mx = sb("mx", [P, 4], F32)
        zt = sb("zt", [P, 2, 4], F32)
        rden = sb("rden", [P, 4], F32)
        stats = sb("stats", [P, T, 6], F32)
        mv = sb("mv", [P, T, 2], F32)
        rstd = sb("rstd", [P, T], F32)
        mask_row = sb("mask_row", [P, N], BF16)
        xr = sb("xr", [P, X_SLOTS, N], F32)
        rr = sb("rr", [P, PAIR, N], F32)
        pr = sb("pr", [P, PAIR, N], F32)
        pt_hi = sb("pt_hi", [P, PAIR, N], F16)
        pt_lo = sb("pt_lo", [P, PAIR, N], F16)
        yq = sb("yq", [P, 4 * F], F32)
        eq = sb("eq", [P, 4 * F], F32)
        ht_hi = sb("ht_hi", [P, KH * P], F16)
        ht_lo = sb("ht_lo", [P, KH * P], F16)
        diag = sb("diag", [P, H, P], F32)
        h0_hi = hs_hi[:, :].rearrange("p (t f) -> p t f", t=T)
        h0_lo = hs_lo[:, :].rearrange("p (t f) -> p t f", t=T)
        h1_hi = hs_hi[:, :].rearrange("p (k n) -> p k n", k=KF)
        h1_lo = hs_lo[:, :].rearrange("p (k n) -> p k n", k=KF)
        o2T, ffT = cat[:, 0:2, :], cat[:, 2:4, :]

        x_in, out_done = sem("x_in"), sem("out_done")
        ones_done = sem("ones_done")
        stats_done, mv_done, rstd_done, yn_done = sem("stats_done"), sem("mv_done"), sem("rstd_done"), sem("yn_done")
        eps_done, pow_done = sem("eps_done"), sem("pow_done")
        h0hi_done, h0_done = sem("h0hi_done"), sem("h0_done")
        z_ps, cat_act, cat_dve = sem("z_ps"), sem("cat_act"), sem("cat_dve")
        x1_ps, x1_done, h1_ps = sem("x1_ps"), sem("x1_done"), sem("h1_ps")
        h1hi_done, h1_done = sem("h1hi_done"), sem("h1_done")
        wh_ps, whhi_done, wh_done = sem("wh_ps"), sem("whhi_done"), sem("wh_done")
        f2c_done, diag_done, bc_ps, f2_ready = sem("f2c_done"), sem("diag_done"), sem("bc_ps"), sem("f2_ready")
        row_done, x_done, zt_done, bias_done = sem("row_done"), sem("x_done"), sem("zt_done"), sem("bias_done")
        r_done, z_done, p_done = sem("r_done"), sem("z_done"), sem("p_done")
        pt_ps, hi_done, lo_done, mm_done = sem("pt_ps"), sem("hi_done"), sem("lo_done"), sem("mm_done")
        rden_done, y_done, exp_done = sem("rden_done"), sem("y_done"), sem("exp_done")
        em1_done, elu_done = sem("em1_done"), sem("elu_done")
        ht_ps, hthi_done, ht_done = sem("ht_ps"), sem("hthi_done"), sem("ht_done")
        proj_ps, valohi_done = sem("proj_ps"), sem("valohi_done")
        o2t_ps, o2t_act, o2t_dve = sem("o2t_ps"), sem("o2t_act"), sem("o2t_dve")
        ff1_ps, ff1_done, ff2_ps = sem("ff1_ps"), sem("ff1_done"), sem("ff2_ps")
        b2_done, beta_done, ffn_done, gam_done, fin_done = sem("b2_done"), sem("beta_done"), sem("ffn_done"), sem("gam_done"), sem("fin_done")

        def segment(eng, b, layer, quad):
            g0 = b * QB + (0 if layer == 1 else QUADS[1])
            nq = QUADS[layer]
            lo, hi = 2, nq - 2
            for q in range(-2, min(lo, nq + 2)):
                quad(g0 + q, q, False)
            if hi > lo:
                with eng.Fori(lo, hi) as l:
                    quad(g0 + l, l, True)
            for q in range(max(lo, hi), nq + 2):
                quad(g0 + q, q, False)

        def live(layer, l, full, d, u=0):
            return full or 0 <= 4 * l + u + d < 4 * QUADS[layer]

        def cols(l, width, size, offset=0):
            return bass.ds(l * width + offset, size)

        held = {e: sem(f"held_{e}") for e in ("pool", "dve")}

        def hold(eng, name, s, value):
            eng.wait_ge(s, value)
            eng.sem_inc(held[name], 1)

        block = ctx.enter_context(nc.Block())

        @block.sync
        def _(sp):
            sp.sem_inc(fin_done, 1)
            sp.sem_inc(out_done, DMA)
            with sp.Fori(0, B) as b:
                sp.wait_ge(fin_done, b + 1)
                sp.dma_start(xx[:, :, :], x[bass.ds(b, 1), :, :].rearrange("b (t p) f -> p (b t) f", p=P)).then_inc(x_in, DMA)
                sp.wait_ge(fin_done, b + 2)
                sp.dma_start(out[bass.ds(b, 1), :, :].rearrange("b (t p) f -> p (b t) f", p=P), yy[:, :, :]).then_inc(out_done, DMA)
            sp.wait_ge(out_done, (B + 1) * DMA)

        @block.gpsimd
        def _(pool):
            nc.gpsimd.memset(val_hi[:, :, :, F:V], 1.0)
            nc.gpsimd.memset(valo_hi[:, :].rearrange("p (t v) -> p t v", t=T)[:, :, F:V], 1.0).then_inc(ones_done, 1)
            pool.sem_inc(z_done, X_SLOTS)

            def rsqrt(count):
                hold(pool, "pool", mv_done, count)
                nc.gpsimd.tensor_scalar(rstd[:, :], mv[:, :, 1], LN_EPS, None, ALU.add).then_inc(eps_done, 1)
                pool.wait_ge(eps_done, count)
                nc.gpsimd.tensor_tensor(rstd[:, :], rstd[:, :], half_neg[:, :], ALU.pow).then_inc(pow_done, 1)

            with pool.Fori(0, B) as b:
                rsqrt(b * 3 + 1)
                hold(pool, "pool", pow_done, b * 3 + 1)
                nc.gpsimd.tensor_scalar(rstd[:, :], rstd[:, :], LN_SCALE, None, ALU.mult).then_inc(rstd_done, 1)
                rsqrt(b * 3 + 2)
                hold(pool, "pool", pow_done, b * 3 + 2)
                nc.gpsimd.tensor_scalar(rstd[:, :], rstd[:, :], LN_SCALE, None, ALU.mult).then_inc(rstd_done, 1)
                for jt in range(T):
                    pool.wait_ge(f2c_done, b * 2 * T + jt + 1)
                    if jt:
                        pool.wait_ge(bc_ps, b * 2 * T + jt)
                    nc.gpsimd.tensor_tensor(diag[:, :, :], ident[:, :].unsqueeze(1).to_broadcast([P, H, P]),
                                            f2c[:, :].unsqueeze(2).to_broadcast([P, H, P]), ALU.mult).then_inc(diag_done, 1)
                nc.gpsimd.tensor_copy(mask_row[:, :], mask_add[:, 0:N]).then_inc(row_done, 1)
                for layer in (1, 2):
                    def quad(g, l, full, layer=layer):
                        n = g * 4
                        for u in range(4):
                            if live(layer, l, full, 2, u):
                                pool.wait_ge(r_done, n + u + 3)
                                nc.gpsimd.tensor_tensor(rr[:, u % PAIR, :], rr[:, u % PAIR, :], xr[:, (u + 2) % X_SLOTS, :],
                                                        ALU.add).then_inc(z_done, 1)
                            if u == 2 and layer == 1 and live(layer, l, full, 8) and live(layer, l, full, 7):
                                hold(pool, "pool", x_done, n + 8)
                                nc.gpsimd.tensor_copy(mask_row[:, :], mask_add[:, cols(l + 2, N, N)]).then_inc(row_done, 1)
                    segment(pool, b, layer, quad)
                pool.wait_ge(o2t_ps, b * 2 + 2)
                nc.gpsimd.tensor_tensor(yy[:, :, :], yy[:, :, :], b2_bc[:, :].unsqueeze(1).to_broadcast([P, T, F]), ALU.add).then_inc(b2_done, 1)
                nc.gpsimd.tensor_tensor(xx[:, :, :], xx[:, :, :], beta_bc[:, :].unsqueeze(1).to_broadcast([P, T, F]), ALU.add).then_inc(beta_done, 1)
                rsqrt(b * 3 + 3)

        @block.scalar
        def _(act):
            act.sem_inc(p_done, PAIR)
            act.wait_ge(ones_done, 1)
            with act.Fori(0, B) as b:
                act.wait_ge(yn_done, b * 3 + 1)
                nc.scalar.activation(hs_hi[:, :], yy[:, :, :].rearrange("p t f -> p (t f)"), ACT.Relu).then_inc(h0hi_done, 1)
                for k in range(KF):
                    act.wait_ge(z_ps, b * 4 + 2 * k + 1)
                    nc.scalar.activation(cat[:, KF + k, :], psum[2 * k][:, :], ACT.Copy, scale=1.0 / LN_SCALE).then_inc(cat_act, 1)
                for k in range(KF):
                    act.wait_ge(h1_ps, b * 2 + k + 1)
                    nc.scalar.activation(h1_hi[:, k, :], psum[2 + k][:, :], ACT.Relu).then_inc(h1hi_done, 1)
                for jt in range(T + 1):
                    if jt < T:
                        act.wait_ge(wh_ps, b * T + jt + 1)
                        nc.scalar.activation(val_hi[:, jt, :, 0:F], psum[jt % 2][:, :].rearrange("p (h f) -> p h f", h=H),
                                             ACT.Copy, scale=VAL_SCALE).then_inc(whhi_done, 1)
                    if jt >= 1:
                        act.wait_ge(bc_ps, b * 2 * T + jt)
                        nc.scalar.activation(cat[:, :, (jt - 1) * P:jt * P], psum[2 + (jt - 1) % 2][:, 512:1024].rearrange("p (h n) -> p h n", h=H),
                                             ACT.Copy).then_inc(f2_ready, 1)
                for layer in (1, 2):
                    def quad(g, l, full, layer=layer):
                        n = g * 4
                        s0 = 0 if layer == 1 else 4 * T

                        def rectify(u):
                            if live(layer, l, full, 2, u):
                                m, dq = (u + 2) % 4, (u + 2) // 4
                                if m == 0:
                                    act.wait_ge(bias_done, g + 3)
                                f1 = f1h if layer == 1 else f1o
                                act.wait_ge(p_done, n + u + 1 + PAIR)
                                nc.scalar.activation(rr[:, m % PAIR, :], xr[:, m, :], ACT.Relu, bias=f1[:, cols(l + dq, 4, 1, m)],
                                                     scale=RATIO).then_inc(r_done, 1)

                        post = layer == 1 and live(layer, l, full, -8)
                        if post:
                            act.wait_ge(ht_ps, b * T + l)
                            act.wait_ge(proj_ps, b * T + l - 1)
                            nc.scalar.activation(ht_hi[:, :], psD[:, :], ACT.Copy, scale=scale(S_H)).then_inc(hthi_done, 1)
                        for u in range(4):
                            if u != 2:
                                rectify(u)
                            if live(layer, l, full, 0, u):
                                act.wait_ge(pt_ps, n + u + 1)
                                act.wait_ge(mm_done, n + u + 1)
                                nc.scalar.activation(pt_hi[:, u % PAIR, :], psum[u % PAIR][:, :], ACT.Copy).then_inc(hi_done, 1)
                            if live(layer, l, full, 1, u):
                                m, dq = (u + 1) % 4, (u + 1) // 4
                                act.wait_ge(z_done, n + u + 2 + X_SLOTS)
                                nc.scalar.activation(pr[:, m % PAIR, :], rr[:, m % PAIR, :], ACT.Exp, bias=shift[:, cols(l + dq, 4, 1, s0 + m)],
                                                     scale=UNIT).then_inc(p_done, 1)
                            if u == 2:
                                rectify(u)
                            if u == 1 and live(layer, l, full, -4):
                                act.wait_ge(y_done, n + PAIR)
                                if layer == 1:
                                    act.wait_ge(ht_ps, b * T + l)
                                nc.scalar.activation(eq[:, :], yq[:, :], ACT.Exp).then_inc(exp_done, 1)
                            if u == 1 and post:
                                act.wait_ge(proj_ps, b * T + l)
                                nc.scalar.activation(valo_hi[:, cols(l - 2, V, F)], psD[:, 0:F], ACT.Copy, scale=VALO_SCALE).then_inc(valohi_done, 1)
                            if u == 2 and post:
                                act.wait_ge(bc_ps, b * 2 * T + T + l - 1)
                                nc.scalar.activation(f2o[:, cols(l - 2, P, P)], psD[:, 512:512 + P], ACT.Copy).then_inc(f2_ready, 1)
                    segment(act, b, layer, quad)
                act.wait_ge(o2t_ps, b * 2 + 1)
                nc.scalar.activation(o2T[:, 0, :], psA[:, :], ACT.Copy).then_inc(o2t_act, 1)
                for k in range(KF):
                    act.wait_ge(ff1_ps, b * 2 + k + 1)
                    nc.scalar.activation(ffT[:, k, :], psum[2 + k][:, :], ACT.Relu, bias=b1_col[:, k:k + 1]).then_inc(ff1_done, 1)

        @block.vector
        def _(dve):
            def layernorm(b, i, src):
                for t in range(T):
                    last = nc.vector.bn_stats(stats[:, t, :], src[:, t, :])
                last.then_inc(stats_done, 1)
                hold(dve, "dve", stats_done, b * 3 + i)
                for t in range(T):
                    last = nc.vector.bn_aggr(mv[:, t, :], stats[:, t, :])
                last.then_inc(mv_done, 1)
                dve.wait_ge(mv_done, b * 3 + i)
                if i < 3:
                    dve.wait_ge(rstd_done, b * 2 + i)
                else:
                    dve.wait_ge(pow_done, b * 3 + i)
                for t in range(T):
                    last = nc.vector.tensor_scalar(yy[:, t, :], src[:, t, :], mv[:, t, 0:1], rstd[:, t:t + 1], ALU.subtract, ALU.mult)
                last.then_inc(yn_done, 1)

            dve.sem_inc(lo_done, PAIR)
            dve.sem_inc(y_done, PAIR)
            dve.sem_inc(bias_done, 1)
            with dve.Fori(0, B) as b:
                dve.wait_ge(x_in, b * DMA + DMA)
                dve.wait_ge(out_done, b * DMA + DMA)
                layernorm(b, 1, xx)
                dve.wait_ge(yn_done, b * 3 + 1)
                dve.wait_ge(h0hi_done, b + 1)
                nc.vector.scalar_tensor_tensor(hs_lo[:, :], yy[:, :, :].rearrange("p t f -> p (t f)"), 0.0, hs_hi[:, :],
                                               ALU.max, ALU.subtract).then_inc(h0_done, 1)
                for t in range(T):
                    last = nc.vector.scalar_tensor_tensor(xx[:, t, :], b0_bc[:, :], deg[:, t:t + 1], xx[:, t, :], ALU.mult, ALU.add)
                last.then_inc(x1_done, 1)
                for k in range(KF):
                    dve.wait_ge(z_ps, b * 4 + 2 * k + 2)
                    nc.vector.tensor_scalar(cat[:, k, :], psum[2 * k + 1][:, :], 1.0 / LN_SCALE, None, ALU.mult).then_inc(cat_dve, 1)
                dve.wait_ge(x1_done, b * 3 + 1)
                for i in range(2):
                    dve.wait_ge(x1_ps, b * 2 + i + 1)
                    half = xx[:, i * T // 2:(i + 1) * T // 2, :]
                    nc.vector.tensor_tensor(half, psum[i][:, :].rearrange("p (t f) -> p t f", f=F), half, ALU.add).then_inc(x1_done, 1)
                dve.wait_ge(x1_done, b * 3 + 3)
                layernorm(b, 2, xx)
                for k in range(KF):
                    dve.wait_ge(h1hi_done, b * 2 + k + 1)
                    nc.vector.scalar_tensor_tensor(h1_lo[:, k, :], psum[2 + k][:, :], 0.0, h1_hi[:, k, :], ALU.max, ALU.subtract).then_inc(h1_done, 1)
                for jt in range(T):
                    side = psum[2 + jt % 2]
                    dve.wait_ge(wh_ps, b * T + jt + 1)
                    if jt:
                        dve.wait_ge(diag_done, b * 2 * T + jt)
                    nc.vector.tensor_scalar(f1h[:, jt * H:(jt + 1) * H], side[:, 0:H], scale(S_F1), None, ALU.mult)
                    nc.vector.tensor_scalar(f2c[:, :], side[:, H:NF], scale(S_F2), None, ALU.mult).then_inc(f2c_done, 1)
                    dve.wait_ge(whhi_done, b * T + jt + 1)
                    nc.vector.scalar_tensor_tensor(val_lo[:, jt, :, 0:F], psum[jt % 2][:, :].rearrange("p (h f) -> p h f", h=H), VAL_SCALE,
                                                   val_hi[:, jt, :, 0:F], ALU.mult, ALU.subtract).then_inc(wh_done, 1)
                for layer in (1, 2):
                    def quad(g, l, full, layer=layer):
                        n = g * 4
                        s0 = 0 if layer == 1 else 4 * T

                        def masked_row(u):
                            if not live(layer, l, full, 5, u):
                                return
                            m, dq = (u + 5) % 4, (u + 5) // 4
                            hold(dve, "dve", bias_done, g + dq + 1)
                            hold(dve, "dve", z_done, n + u + 6)
                            if layer == 1:
                                if m == 0:
                                    if not full and l == -2:
                                        hold(dve, "dve", f2_ready, b * 2 * T + T)
                                    hold(dve, "dve", row_done, b * T + l + 3)
                                row, f2 = mask_row[:, :], cat[:, m, :]
                            else:
                                if m == 0 and l == -2:
                                    hold(dve, "dve", f2_ready, b * 2 * T + 2 * T)
                                tile = 4 * (l + dq) + m
                                row, f2 = mask_add[:, tile * N:(tile + 1) * N], f2o[:, :]
                            nc.vector.tensor_tensor_reduce(out=xr[:, m, :], in0=f2, in1=row, scale=1.0, scalar=MASKED * 2,
                                                           op0=ALU.add, op1=ALU.max, accum_out=mx[:, m:m + 1]).then_inc(x_done, 1)

                        def maxima():
                            f1 = (f1h if layer == 1 else f1o)[:, cols(l + 1, 4, 4)]
                            dve.wait_ge(x_done, n + 8)
                            nc.vector.scalar_tensor_tensor(zt[:, 0, :], mx[:, :], RATIO, f1, ALU.mult, ALU.add).then_inc(zt_done, 1)
                            dve.wait_ge(zt_done, g * 2 + 3)
                            nc.vector.scalar_tensor_tensor(zt[:, 1, :], zt[:, 0, :], 0.0, mx[:, :], ALU.max, ALU.add).then_inc(zt_done, 1)
                            dve.wait_ge(zt_done, g * 2 + 4)
                            nc.vector.tensor_scalar(shift[:, cols(l + 1, 4, 4, s0)], zt[:, 1, :], -UNIT, None, ALU.mult).then_inc(bias_done, 1)

                        post = layer == 1 and live(layer, l, full, -8)
                        if post:
                            dve.wait_ge(hthi_done, b * T + l - 1)
                            nc.vector.scalar_tensor_tensor(ht_lo[:, :], psD[:, :], scale(S_H), ht_hi[:, :], ALU.mult, ALU.subtract).then_inc(ht_done, 1)
                        for u in range(4):
                            if u == 2:
                                masked_row(u)
                                if live(layer, l, full, 4):
                                    maxima()
                            if live(layer, l, full, -1, u):
                                k = (u - 1) % PAIR
                                dve.wait_ge(hi_done, n + u)
                                nc.vector.tensor_tensor(pt_lo[:, k, :], psum[k][:, :], pt_hi[:, k, :], ALU.subtract).then_inc(lo_done, 1)
                            if u != 2:
                                masked_row(u)
                            if u == 2 and live(layer, l, full, -4):
                                dve.wait_ge(exp_done, g)
                                nc.vector.tensor_scalar(eq[:, :], eq[:, :], 1.0, -1.0, ALU.min, ALU.add).then_inc(em1_done, 1)
                                dve.wait_ge(em1_done, g)
                                to = eq[:, :] if layer == 1 else yy[:, 4 * (l - 1):4 * l, :].rearrange("p t f -> p (t f)")
                                nc.vector.scalar_tensor_tensor(to, yq[:, :], 0.0, eq[:, :], ALU.max, ALU.add).then_inc(elu_done, 1)
                            if live(layer, l, full, -2, u):
                                k = (u - 2) % 4
                                o = psC[:, (k % PAIR) * 512:(k % PAIR) * 512 + F + 1]
                                dve.wait_ge(mm_done, n + u - 1 + PAIR)
                                nc.vector.reciprocal(rden[:, k:k + 1], o[:, F:F + 1]).then_inc(rden_done, 1)
                                dve.wait_ge(rden_done, n + u - 1)
                                nc.vector.tensor_scalar(yq[:, k * F:(k + 1) * F], o[:, 0:F], rden[:, k:k + 1], scale(S_HINV if layer == 1 else S_OINV),
                                                        ALU.mult, ALU.mult).then_inc(y_done, 1)
                            if u == 1 and post:
                                dve.wait_ge(valohi_done, b * T + l - 1)
                                nc.vector.scalar_tensor_tensor(valo_lo[:, cols(l - 2, V, F)], psD[:, 0:F], VALO_SCALE, valo_hi[:, cols(l - 2, V, F)],
                                                               ALU.mult, ALU.subtract)
                                nc.vector.tensor_scalar(f1o[:, cols(l - 2, 1, 1)], psD[:, F:F + 1], scale(S_FO1), None, ALU.mult)
                                nc.vector.tensor_scalar(f2oc[:, :], psD[:, F + 1:F + 2], scale(S_FO2), None, ALU.mult).then_inc(f2c_done, 1)
                                dve.wait_ge(f2c_done, b * 2 * T + T + l - 1)
                                nc.vector.tensor_scalar(diag[:, 0, :], ident[:, :], f2oc[:, :], None, ALU.mult).then_inc(diag_done, 1)
                    segment(dve, b, layer, quad)
                dve.wait_ge(o2t_ps, b * 2 + 2)
                nc.vector.tensor_copy(o2T[:, 1, :], psB[:, :]).then_inc(o2t_dve, 1)
                dve.wait_ge(b2_done, b + 1)
                for i in range(2):
                    dve.wait_ge(ff2_ps, b * 2 + i + 1)
                    half = yy[:, i * T // 2:(i + 1) * T // 2, :]
                    nc.vector.tensor_tensor(half, psum[i][:, :].rearrange("p (t f) -> p t f", f=F), half, ALU.add).then_inc(ffn_done, 1)
                dve.wait_ge(ffn_done, b * 2 + 2)
                layernorm(b, 3, yy)
                dve.wait_ge(yn_done, b * 3 + 3)
                nc.vector.tensor_tensor(yy[:, :, :], yy[:, :, :], gamma_bc[:, :].unsqueeze(1).to_broadcast([P, T, F]), ALU.mult).then_inc(gam_done, 1)
                dve.wait_ge(gam_done, b + 1)
                dve.wait_ge(beta_done, b + 1)
                nc.vector.tensor_tensor(yy[:, :, :], yy[:, :, :], xx[:, :, :], ALU.add).then_inc(fin_done, 1)

        @block.tensor
        def _(pe):
            def product(to, wide, pairs, start_to=None):
                for i, (lhsT, rhs) in enumerate(pairs):
                    last = nc.tensor.matmul(to, lhsT, rhs, start=i == 0, stop=i == len(pairs) - 1)
                return last

            pe.sem_inc(mm_done, PAIR)
            pe.sem_inc(ht_ps, 1)
            pe.sem_inc(proj_ps, 1)
            with pe.Fori(0, B) as b:
                pe.wait_ge(h0hi_done, b + 1)
                pe.wait_ge(h0_done, b + 1)
                for k in range(KF):
                    fk = slice(k * P, (k + 1) * P)
                    for c in range(2):
                        last = product(psum[2 * k][:, c * 512:(c + 1) * 512], 512,
                                       [(h[:, jt, fk], adjT[:, jt, c * 512:(c + 1) * 512]) for jt in range(T) for h in (h0_hi, h0_lo)])
                    last.then_inc(z_ps, 1)
                    for t in range(T):
                        last = product(psum[2 * k + 1][:, t * P:(t + 1) * P], P, [(h[:, t, fk], diag_deg[:, t, :]) for h in (h0_hi, h0_lo)])
                    last.then_inc(z_ps, 1)
                pe.wait_ge(cat_act, b * 2 + 2)
                pe.wait_ge(cat_dve, b * 2 + 2)
                for i in range(2):
                    for t in range(T // 2):
                        tok = slice((i * 4 + t) * P, (i * 4 + t + 1) * P)
                        last = product(psum[i][:, t * F:(t + 1) * F], F, [(cat[:, k, tok], w0T[:, k, :]) for k in range(4)])
                    last.then_inc(x1_ps, 1)
                pe.wait_ge(yn_done, b * 3 + 2)
                for k in range(KF):
                    for t in range(T):
                        last = nc.tensor.transpose(psum[2 + k][:, t * P:(t + 1) * P], yy[:, t, k * P:(k + 1) * P], ident[:, :])
                    last.then_inc(h1_ps, 1)
                pe.wait_ge(h1_done, b * 2 + 2)
                for jt in range(T + 1):
                    if jt < T:
                        tok = slice(jt * P, (jt + 1) * P)
                        if jt >= 2:
                            pe.wait_ge(wh_done, b * T + jt - 1)
                            pe.wait_ge(f2_ready, b * 2 * T + jt - 1)
                        three = [(h1_hi, wh_hi), (h1_hi, wh_lo), (h1_lo, wh_hi)]
                        for c in range(2):
                            product(psum[jt % 2][:, c * 512:(c + 1) * 512], 512,
                                    [(h[:, k, tok], w[:, k, c * 512:(c + 1) * 512]) for k in range(KF) for h, w in three])
                        product(psum[2 + jt % 2][:, 0:NF], NF, [(h[:, k, tok], w[:, k, HF:HF + NF]) for k in range(KF) for h, w in three]).then_inc(wh_ps, 1)
                    if jt >= 1:
                        pe.wait_ge(diag_done, b * 2 * T + jt)
                        nc.tensor.matmul(psum[2 + (jt - 1) % 2][:, 512:1024], ones[:, :], diag[:, :, :].rearrange("p h n -> p (h n)"),
                                         start=True, stop=True).then_inc(bc_ps, 1)
                for layer in (1, 2):
                    def quad(g, l, full, layer=layer):
                        n = g * 4
                        for u in range(4):
                            if u == 2 and layer == 1 and live(layer, l, full, -8):
                                pe.wait_ge(diag_done, b * 2 * T + T + l - 1)
                                nc.tensor.matmul(psD[:, 512:512 + P], ones[:, :], diag[:, 0, :], start=True, stop=True).then_inc(bc_ps, 1)
                            if live(layer, l, full, 0, u):
                                pe.wait_ge(p_done, n + u + 1 + PAIR)
                                pe.wait_ge(lo_done, n + u + 1)
                                for t in range(T):
                                    last = nc.tensor.transpose(psum[u % PAIR][:, t * P:(t + 1) * P], pr[:, u % PAIR, t * P:(t + 1) * P], ident[:, :])
                                last.then_inc(pt_ps, 1)
                            if live(layer, l, full, -1, u):
                                m = (u - 1) % 4
                                o = psC[:, (m % PAIR) * 512:(m % PAIR) * 512 + 512]
                                hi, lo = pt_hi[:, m % PAIR, :], pt_lo[:, m % PAIR, :]
                                pe.wait_ge(y_done, n + u)
                                pe.wait_ge(hi_done, n + u)
                                for t in range(T):
                                    vh = val_hi[:, t, m, 0:F + 1] if layer == 1 else valo_hi[:, t * V:t * V + F + 1]
                                    vl = val_lo[:, t, m, 0:F] if layer == 1 else valo_lo[:, t * V:t * V + F]
                                    nc.tensor.matmul(o[:, 0:F + 1], hi[:, t * P:(t + 1) * P], vh, start=t == 0, stop=False)
                                    nc.tensor.matmul(o[:, 0:F], hi[:, t * P:(t + 1) * P], vl, start=False, stop=False)
                                pe.wait_ge(lo_done, n + u + PAIR)
                                for t in range(T):
                                    vh = val_hi[:, t, m, 0:F + 1] if layer == 1 else valo_hi[:, t * V:t * V + F + 1]
                                    last = nc.tensor.matmul(o[:, 0:F + 1], lo[:, t * P:(t + 1) * P], vh, start=False, stop=t == T - 1)
                                last.then_inc(mm_done, 1)
                            if u == 0 and layer == 1 and live(layer, l, full, -8):
                                pe.wait_ge(ht_done, b * T + l - 1)
                                product(psD[:, 0:V], V, [(h[:, k * P:(k + 1) * P], w[:, k, :]) for k in range(KH)
                                                         for h, w in ((ht_hi, wo_hi), (ht_hi, wo_lo), (ht_lo, wo_hi))]).then_inc(proj_ps, 1)
                            if u == 3 and layer == 1 and live(layer, l, full, -4):
                                pe.wait_ge(elu_done, g)
                                pe.wait_ge(f2_ready, b * 2 * T + T + l - 1)
                                for k in range(KH):
                                    last = nc.tensor.transpose(psD[:, k * P:(k + 1) * P], eq[:, k * P:(k + 1) * P], ident[:, :])
                                last.then_inc(ht_ps, 1)
                    segment(pe, b, layer, quad)
                pe.wait_ge(elu_done, b * QB + QB)
                for k in range(KF):
                    for t in range(T):
                        last = nc.tensor.transpose(psum[k][:, t * P:(t + 1) * P], yy[:, t, k * P:(k + 1) * P], ident[:, :])
                    last.then_inc(o2t_ps, 1)
                pe.wait_ge(o2t_act, b + 1)
                pe.wait_ge(o2t_dve, b + 1)
                for m in range(KF):
                    for c in range(2):
                        last = product(psum[2 + m][:, c * 512:(c + 1) * 512], 512,
                                       [(w1_sb[:, k, m * P:(m + 1) * P], o2T[:, k, c * 512:(c + 1) * 512]) for k in range(KF)])
                    last.then_inc(ff1_ps, 1)
                pe.wait_ge(ff1_done, b * 2 + 2)
                for i in range(2):
                    for t in range(T // 2):
                        tok = slice((i * 4 + t) * P, (i * 4 + t + 1) * P)
                        last = product(psum[i][:, t * F:(t + 1) * F], F, [(ffT[:, k, tok], w2_sb[:, k, :]) for k in range(KF)])
                    last.then_inc(ff2_ps, 1)


_INS = ['x', 'adj', 'L0_gnn_W', 'L0_gnn_b', 'L1_gnn_W_heads', 'L1_gnn_a_heads', 'L1_gnn_W_out', 'L1_gnn_a_out',
        'L1_gnn_w1', 'L1_gnn_b1', 'L1_gnn_w2', 'L1_gnn_b2', 'L1_gnn_ln_gamma', 'L1_gnn_ln_beta']


def kernel(**inputs):
    import numpy as np
    import concourse.bacc as bacc
    from concourse.bass_utils import run_bass_kernel_spmd

    nc = bacc.Bacc("TRN2", target_bir_lowering=False, num_devices=1)
    arrays, args = {}, []
    for name in _INS:
        a = np.ascontiguousarray(inputs[name])
        arrays[f"in_{name}"] = a
        args.append(nc.dram_tensor(f"in_{name}", a.shape, mybir.dt.from_np(a.dtype), kind="ExternalInput").ap())
    out = nc.dram_tensor("out", arrays["in_x"].shape, F32, kind="ExternalOutput").ap()
    build(nc, *args, out)
    r = run_bass_kernel_spmd(nc, [arrays], core_ids=[0])
    return r.results[0]["out"]
```

```python
from contextlib import ExitStack

import concourse.bass as bass
from concourse import mybir

ALU = mybir.AluOpType
ACT = mybir.ActivationFunctionType
F32, F16, BF16, I32 = mybir.dt.float32, mybir.dt.float16, mybir.dt.bfloat16, mybir.dt.int32
AX = mybir.AxisListType.X

P = 128
LN_EPS = 1e-5
ALPHA = 0.01
UNIT = 2.0 ** -7
LIN = ALPHA / UNIT
STEP = (1.0 - ALPHA) / UNIT
RATIO = (1.0 - ALPHA) / ALPHA
MASKED = -(2.0 ** 100)
LN_LOG = 11
W_LOG = 13
LN_SCALE = 2.0 ** LN_LOG
WH_LOG = 15 - 4
VAL_SCALE = 2.0 ** (WH_LOG - LN_LOG - W_LOG)
VALO_SCALE = 2.0 ** (6 - WH_LOG - W_LOG)
X_SLOTS = 4
PAIR = 2


def build(nc, x, adj, w0, b0, w_heads, a_heads, w_out, a_out, w1, b1, w2, b2, gamma, beta, out):
    B, N, F = x.shape
    H = w_heads.shape[0]
    T = N // P
    KF = F // P
    HF = H * F
    KH = HF // P
    V = F + 2
    NF = 2 * H
    assert H == 4 and T == 8 and KF == 2 and HF == N
    QUADS = {1: T, 2: T // 4}
    UB = 4 * (QUADS[1] + QUADS[2])
    QB = QUADS[1] + QUADS[2]
    DMA = 16

    with ExitStack() as ctx:
        def sb(name, shape, dt, stack=ctx):
            return stack.enter_context(nc.sbuf_tensor(name, shape, dt))

        def sem(name):
            return ctx.enter_context(nc.semaphore(name))

        mask_add = sb("mask_add", [P, T * N], BF16)
        adjT = sb("adjT", [P, T, N], F16)
        diag_deg = sb("diag_deg", [P, T, P], F16)
        deg = sb("deg", [P, T], F32)
        w0T = sb("w0T", [P, 2 * KF, F], F32)
        wh_hi = sb("wh_hi", [P, KF, HF + NF], F16)
        wh_lo = sb("wh_lo", [P, KF, HF + NF], F16)
        wo_hi = sb("wo_hi", [P, KH, V], F16)
        wo_lo = sb("wo_lo", [P, KH, V], F16)
        w1_sb = sb("w1_sb", [P, KF, F], F32)
        w2_sb = sb("w2_sb", [P, KF, F], F32)
        b1_col = sb("b1_col", [P, KF], F32)
        b0_bc = sb("b0_bc", [P, F], F32)
        b2_bc = sb("b2_bc", [P, F], F32)
        gamma_bc = sb("gamma_bc", [P, F], F32)
        beta_bc = sb("beta_bc", [P, F], F32)
        ident = sb("ident", [P, P], F32)
        ident16 = sb("ident16", [P, P], F16)
        ones = sb("ones", [P, P], F32)
        half_neg = sb("half_neg", [P, T], F32)
        sc = sb("sc", [P, 16], F32)
        S_WH, S_WO, S_WA, S_WAO, S_F, S_H, S_HINV, S_OINV, S_FO, S_F1, S_F2, S_FO1, S_FO2 = range(13)

        def scale(i):
            return sc[:, i:i + 1]

        psum = [ctx.enter_context(nc.psum_tensor(f"ps{i}", [P, 1024], F32)) for i in range(4)]
        psA, psB, psC, psD = psum

        with ExitStack() as tmp:
            adj_i = sb("adj_i", [P, T, N], I32, tmp)
            adj16 = sb("adj16", [P, T, N], F16, tmp)
            w0_sb = sb("w0_sb", [P, KF, 2 * F], F32, tmp)
            whf = sb("whf", [P, KF, H, F], F32, tmp)
            wof = sb("wof", [P, KH, F], F32, tmp)
            ah_bc = sb("ah_bc", [P, H, 2, F], F32, tmp)
            ao_bc = sb("ao_bc", [P, 2, F], F32, tmp)
            waf = sb("waf", [P, KF, 2, H], F32, tmp)
            wao = sb("wao", [P, KH, 2], F32, tmp)
            sq = sb("sq", [P, KF * HF], F32, tmp)
            sqo = sb("sqo", [P, KH * F], F32, tmp)
            sqa = sb("sqa", [P, 32], F32, tmp)
            nsq = sb("nsq", [P, 4], F32, tmp)
            ei = sb("ei", [P, 4], I32, tmp)
            ki = sb("ki", [P, 4], I32, tmp)
            kf = sb("kf", [P, 4], F32, tmp)
            ksum = sb("ksum", [P, 2], F32, tmp)
            ebits = sb("ebits", [P, 16], F32, tmp)
            eint = sb("eint", [P, 16], I32, tmp)
            adj_in, w_in, a_in, c_in = sem("adj_in"), sem("w_in"), sem("a_in"), sem("c_in")
            zero_done, ident_done = sem("zero_done"), sem("ident_done")
            adj16_done, sq_done, norm_done = sem("adj16_done"), sem("sq_done"), sem("norm_done")
            at_done, at_copied, w0t_done = sem("at_done"), sem("at_copied"), sem("w0t_done")
            setup_dve = sem("setup_dve")
            with nc.Block() as block:
                @block.sync
                def _(sp):
                    sp.dma_start(adj_i[:, 0:T // 2, :], adj[0:N // 2, :].rearrange("(t p) j -> p t j", p=P)).then_inc(adj_in, DMA)
                    sp.dma_start(adj_i[:, T // 2:T, :], adj[N // 2:N, :].rearrange("(t p) j -> p t j", p=P)).then_inc(adj_in, DMA)
                    sp.dma_start(b0_bc[:, :], b0.partition_broadcast(P)).then_inc(c_in, DMA)
                    sp.dma_start(b2_bc[:, :], b2.partition_broadcast(P)).then_inc(c_in, DMA)
                    sp.dma_start(gamma_bc[:, :], gamma.partition_broadcast(P)).then_inc(c_in, DMA)
                    sp.dma_start(beta_bc[:, :], beta.partition_broadcast(P)).then_inc(c_in, DMA)
                    sp.dma_start(b1_col[:, :], b1.rearrange("(k p) -> p k", p=P), allow_slow_non_contiguous=True).then_inc(c_in, DMA)
                    sp.dma_start(w1_sb[:, :, :], w1.rearrange("(k p) n -> p k n", p=P)).then_inc(c_in, DMA)
                    sp.dma_start(w2_sb[:, :, :], w2.rearrange("(k p) n -> p k n", p=P)).then_inc(c_in, DMA)
                    sp.wait_ge(c_in, 7 * DMA)

                @block.scalar
                def _(act):
                    for k in range(KF):
                        act.dma_start(whf[:, k, :, :], w_heads[:, k * P:(k + 1) * P, :].rearrange("h p f -> p h f")).then_inc(w_in, DMA)
                    act.dma_start(wof[:, :, :], w_out.rearrange("(k p) n -> p k n", p=P)).then_inc(w_in, DMA)
                    act.dma_start(w0_sb[:, :, :], w0.rearrange("(k p) n -> p k n", p=P)).then_inc(w_in, DMA)
                    act.dma_start(ah_bc[:, :, :, :].rearrange("p h c f -> p (h c f)"), a_heads.rearrange("h c -> (h c)").partition_broadcast(P)).then_inc(a_in, DMA)
                    act.dma_start(ao_bc[:, :, :].rearrange("p c f -> p (c f)"), a_out.partition_broadcast(P)).then_inc(a_in, DMA)
                    for jt in range(T):
                        act.wait_ge(at_done, jt + 1)
                        nc.scalar.activation(adjT[:, jt, :], psum[jt % 2][:, 0:N // 2].bitcast(F16), ACT.Copy).then_inc(at_copied, 1)
                    act.wait_ge(w0t_done, 1)
                    nc.scalar.activation(w0T[:, :, :].rearrange("p k n -> p (k n)"), psC[:, :], ACT.Copy).then_inc(at_copied, 1)

                @block.gpsimd
                def _(pool):
                    nc.gpsimd.memset(ident[:, :], 0.0).then_inc(zero_done, 1)
                    nc.gpsimd.memset(ident16[:, :], 0.0).then_inc(zero_done, 1)
                    nc.gpsimd.memset(half_neg[:, :], -0.5)
                    nc.gpsimd.memset(ones[:, :], 1.0)
                    pool.wait_ge(zero_done, 2)
                    for m in (ident, ident16):
                        nc.gpsimd.affine_select(out=m[:, :], in_=m[:, :], compare_op=ALU.not_equal, fill=1.0, base=0,
                                                pattern=[[-1, P]], channel_multiplier=1).then_inc(ident_done, 1)

                @block.vector
                def _(dve):
                    chain = [0]

                    def link(instruction):
                        chain[0] += 1
                        instruction.then_inc(setup_dve, 1)
                        dve.wait_ge(setup_dve, chain[0])

                    for half in range(2):
                        t0 = half * T // 2
                        dve.wait_ge(adj_in, 2 * DMA)
                        nc.vector.tensor_copy(adj16[:, t0:t0 + T // 2, :], adj_i[:, t0:t0 + T // 2, :]).then_inc(adj16_done, 1)
                    dve.wait_ge(adj16_done, 2)
                    nc.vector.tensor_scalar(mask_add[:, :], adj16[:, :, :].rearrange("p t j -> p (t j)"), 0.0, MASKED, ALU.is_le, ALU.mult)
                    link(nc.vector.reduce_sum(deg[:, :], adj16[:, :, :], axis=AX))
                    dve.wait_ge(w_in, 4 * DMA)
                    dve.wait_ge(a_in, 2 * DMA)
                    for c in range(2):
                        for k in range(KF):
                            for h in range(H):
                                link(nc.vector.tensor_tensor_reduce(out=sq[:, 0:F], in0=whf[:, k, h, :], in1=ah_bc[:, h, c, :], scale=1.0, scalar=0.0,
                                                                    op0=ALU.mult, op1=ALU.add, accum_out=waf[:, k, c, h:h + 1]))
                        for k in range(KH):
                            link(nc.vector.tensor_tensor_reduce(out=sq[:, 0:F], in0=wof[:, k, :], in1=ao_bc[:, c, :], scale=1.0, scalar=0.0,
                                                                op0=ALU.mult, op1=ALU.add, accum_out=wao[:, k, c:c + 1]))
                    whf_flat = whf[:, :, :, :].rearrange("p k h f -> p (k h f)")
                    wof_flat = wof[:, :, :].rearrange("p k f -> p (k f)")
                    waf_flat = waf[:, :, :, :].rearrange("p k c h -> p (k c h)")
                    wao_flat = wao[:, :, :].rearrange("p k c -> p (k c)")
                    nc.vector.tensor_tensor(sq[:, :], whf_flat, whf_flat, ALU.mult)
                    nc.vector.tensor_tensor(sqo[:, :], wof_flat, wof_flat, ALU.mult)
                    nc.vector.tensor_tensor(sqa[:, 0:16], waf_flat, waf_flat, ALU.mult)
                    nc.vector.tensor_tensor(sqa[:, 16:32], wao_flat, wao_flat, ALU.mult).then_inc(sq_done, 1)
                    dve.wait_ge(ident_done, 2)
                    for t in range(T):
                        last = nc.vector.tensor_scalar(diag_deg[:, t, :], ident16[:, :], deg[:, t:t + 1], None, ALU.mult)
                    dve.wait_ge(norm_done, 1)
                    nc.vector.reduce_max(nsq[:, 0:1], psA[:, :], axis=AX)
                    nc.vector.reduce_max(nsq[:, 1:2], psB[:, 0:F], axis=AX)
                    nc.vector.reduce_max(nsq[:, 2:3], psD[:, 0:NF], axis=AX)
                    link(nc.vector.reduce_max(nsq[:, 3:4], psD[:, NF:NF + 2], axis=AX))
                    link(nc.vector.tensor_scalar(ei[:, :], nsq[:, :].bitcast(I32), 23, None, ALU.logical_shift_right))
                    link(nc.vector.tensor_scalar(ei[:, :], ei[:, :], 129.0, None, ALU.add))
                    link(nc.vector.tensor_scalar(ki[:, :], ei[:, :], 1, None, ALU.logical_shift_right))
                    link(nc.vector.tensor_copy(kf[:, :], ki[:, :]))
                    nc.vector.tensor_tensor(ksum[:, 0:1], kf[:, 0:1], kf[:, 1:2], ALU.add)
                    link(nc.vector.tensor_tensor(ksum[:, 1:2], kf[:, 0:1], kf[:, 3:4], ALU.add))
                    link(nc.vector.memset(ebits[:, :], 127.0))
                    nc.vector.tensor_scalar(ebits[:, 0:4], kf[:, 0:4], -1.0, 254.0 + W_LOG, ALU.mult, ALU.add)
                    nc.vector.tensor_scalar(ebits[:, S_F:S_F + 1], kf[:, 2:3], -float(LN_LOG + W_LOG), None, ALU.add)
                    nc.vector.tensor_scalar(ebits[:, S_H:S_H + 1], kf[:, 0:1], -1.0, 254.0 + WH_LOG, ALU.mult, ALU.add)
                    nc.vector.tensor_scalar(ebits[:, S_HINV:S_HINV + 1], kf[:, 0:1], -float(WH_LOG), None, ALU.add)
                    nc.vector.tensor_scalar(ebits[:, S_OINV:S_OINV + 1], ksum[:, 0:1], -127.0 - 6.0, None, ALU.add)
                    link(nc.vector.tensor_scalar(ebits[:, S_FO:S_FO + 1], ksum[:, 1:2], -127.0 - float(WH_LOG + W_LOG), None, ALU.add))
                    link(nc.vector.tensor_scalar(eint[:, :], ebits[:, :], 1.0, 254.0, ALU.max, ALU.min))
                    link(nc.vector.tensor_scalar(sc[:, :].bitcast(I32), eint[:, :], 23, None, ALU.logical_shift_left))
                    nc.vector.tensor_scalar(scale(S_F1), scale(S_F), STEP, None, ALU.mult)
                    nc.vector.tensor_scalar(scale(S_F2), scale(S_F), LIN, None, ALU.mult)
                    nc.vector.tensor_scalar(scale(S_FO1), scale(S_FO), STEP, None, ALU.mult)
                    nc.vector.tensor_scalar(scale(S_FO2), scale(S_FO), LIN, None, ALU.mult)
                    for src, hi, lo, s in (
                        (whf[:, :, :, :].rearrange("p k h f -> p k (h f)"), wh_hi[:, :, 0:HF], wh_lo[:, :, 0:HF], S_WH),
                        (waf[:, :, :, :].rearrange("p k c h -> p k (c h)"), wh_hi[:, :, HF:HF + NF], wh_lo[:, :, HF:HF + NF], S_WA),
                        (wof[:, :, :], wo_hi[:, :, 0:F], wo_lo[:, :, 0:F], S_WO),
                        (wao[:, :, :], wo_hi[:, :, F:V], wo_lo[:, :, F:V], S_WAO),
                    ):
                        link(nc.vector.tensor_scalar(hi, src, scale(s), None, ALU.mult))
                        link(nc.vector.scalar_tensor_tensor(lo, src, scale(s), hi, ALU.mult, ALU.subtract))

                @block.tensor
                def _(pe):
                    pe.wait_ge(ident_done, 2)
                    pe.wait_ge(w_in, 4 * DMA)
                    for k in range(2 * KF):
                        for o in range(KF):
                            last = nc.tensor.transpose(psC[:, k * F + o * P:k * F + (o + 1) * P], w0_sb[:, o, k * P:(k + 1) * P], ident[:, :])
                    last.then_inc(w0t_done, 1)
                    pe.wait_ge(adj16_done, 2)
                    for jt in range(T):
                        if jt >= 2:
                            pe.wait_ge(at_copied, jt - 1)
                        for it in range(T):
                            last = nc.tensor.transpose(psum[jt % 2][:, it * P // 2:(it + 1) * P // 2].bitcast(F16),
                                                       adj16[:, it, jt * P:(jt + 1) * P], ident16[:, :])
                        last.then_inc(at_done, 1)
                    pe.wait_ge(at_copied, T)
                    pe.wait_ge(sq_done, 1)
                    for c in range(2):
                        for k in range(KF):
                            nc.tensor.matmul(psA[:, c * 512:(c + 1) * 512], ones[:, :], sq[:, k * HF + c * 512:k * HF + (c + 1) * 512],
                                             start=k == 0, stop=k == KF - 1)
                    for k in range(KH):
                        nc.tensor.matmul(psB[:, 0:F], ones[:, :], sqo[:, k * F:(k + 1) * F], start=k == 0, stop=k == KH - 1)
                    for k in range(KF):
                        nc.tensor.matmul(psD[:, 0:NF], ones[:, :], sqa[:, k * NF:(k + 1) * NF], start=k == 0, stop=k == KF - 1)
                    for k in range(KH):
                        last = nc.tensor.matmul(psD[:, NF:NF + 2], ones[:, :], sqa[:, 16 + 2 * k:18 + 2 * k], start=k == 0, stop=k == KH - 1)
                    last.then_inc(norm_done, 1)

        xx = sb("xx", [P, T, F], F32)
        yy = sb("yy", [P, T, F], F32)
        hs_hi = sb("hs_hi", [P, 2048], F16)
        hs_lo = sb("hs_lo", [P, 2048], F16)
        cat = sb("cat", [P, 4, N], F32)
        val_hi = sb("val_hi", [P, T, H, V], F16)
        val_lo = sb("val_lo", [P, T, H, V], F16)
        valo_hi = sb("valo_hi", [P, T * V], F16)
        valo_lo = sb("valo_lo", [P, T * V], F16)
        f2o = sb("f2o", [P, N], F32)
        f1h = sb("f1h", [P, T * H], F32)
        f1o = sb("f1o", [P, T], F32)
        f2c = sb("f2c", [P, H], F32)
        f2oc = sb("f2oc", [P, 1], F32)
        shift = sb("shift", [P, (T + 2) * 4], F32)
        mx = sb("mx", [P, 4], F32)
        zt = sb("zt", [P, 2, 4], F32)
        rden = sb("rden", [P, 4], F32)
        stats = sb("stats", [P, T, 6], F32)
        mv = sb("mv", [P, T, 2], F32)
        rstd = sb("rstd", [P, T], F32)
        mask_row = sb("mask_row", [P, N], BF16)
        xr = sb("xr", [P, X_SLOTS, N], F32)
        rr = sb("rr", [P, PAIR, N], F32)
        pr = sb("pr", [P, PAIR, N], F32)
        pt_hi = sb("pt_hi", [P, PAIR, N], F16)
        pt_lo = sb("pt_lo", [P, PAIR, N], F16)
        yq = sb("yq", [P, 4 * F], F32)
        eq = sb("eq", [P, 4 * F], F32)
        ht = sb("ht", [P, 2 * KH * P], F16)
        ht_hi, ht_lo = ht[:, 0:KH * P], ht[:, KH * P:2 * KH * P]
        diag = sb("diag", [P, H, P], F32)
        h0_hi = hs_hi[:, :].rearrange("p (t f) -> p t f", t=T)
        h0_lo = hs_lo[:, :].rearrange("p (t f) -> p t f", t=T)
        h1_hi = hs_hi[:, :].rearrange("p (k n) -> p k n", k=KF)
        h1_lo = hs_lo[:, :].rearrange("p (k n) -> p k n", k=KF)
        o2 = [ht[:, :].bitcast(F32), f2o[:, :]]
        o2t = [o.rearrange("p (t f) -> p t f", f=F) for o in o2]
        o2T = yy[:, :, :].rearrange("p t f -> p (t f)").rearrange("p (k n) -> p k n", k=KF)
        ffT = [hs_hi[:, :].bitcast(F32), hs_lo[:, :].bitcast(F32)]
        x1_dram = nc.dram_tensor("x1_rows", [B, N, F], F32).ap()

        LN_X, LN_X1, LN_Y = "x", "x1", "y"
        stats_done = {i: sem(f"stats_done_{i}") for i in (LN_X, LN_X1, LN_Y)}
        mv_done = {i: sem(f"mv_done_{i}") for i in (LN_X, LN_X1, LN_Y)}
        eps_done = {i: sem(f"eps_done_{i}") for i in (LN_X, LN_X1, LN_Y)}
        pow_done = {i: sem(f"pow_done_{i}") for i in (LN_X, LN_X1, LN_Y)}
        rstd_done = {i: sem(f"rstd_done_{i}") for i in (LN_X, LN_X1)}
        yn_done = {i: sem(f"yn_done_{i}") for i in (LN_X, LN_X1, LN_Y)}
        x_in, x1_saved, x1_back, out_done = sem("x_in"), sem("x1_saved"), sem("x1_back"), sem("out_done")
        ones_done = sem("ones_done")
        h0hi_done, h0_done = sem("h0hi_done"), sem("h0_done")
        z_ps, cat_act, cat_dve = sem("z_ps"), sem("cat_act"), sem("cat_dve")
        x1_ps, x1_done, h1_ps = sem("x1_ps"), sem("x1_done"), sem("h1_ps")
        h1hi_done, h1_done = sem("h1hi_done"), sem("h1_done")
        wh_ps, whhi_done, wh_done = sem("wh_ps"), sem("whhi_done"), sem("wh_done")
        f2c_done, diag_done, bc_ps, f2_ready = sem("f2c_done"), sem("diag_done"), sem("bc_ps"), sem("f2_ready")
        row_done, x_done, zt_done, bias_done = sem("row_done"), sem("x_done"), sem("zt_done"), sem("bias_done")
        r_done, z_done, p_done = sem("r_done"), sem("z_done"), sem("p_done")
        pt_ps, hi_done, lo_done, mm_done = sem("pt_ps"), sem("hi_done"), sem("lo_done"), sem("mm_done")
        rden_done, y_done, exp_done = sem("rden_done"), sem("y_done"), sem("exp_done")
        em1_done, elu_done = sem("em1_done"), sem("elu_done")
        ht_ps, hthi_done, ht_done = sem("ht_ps"), sem("hthi_done"), sem("ht_done")
        proj_ps, valohi_done = sem("proj_ps"), sem("valohi_done")
        o2t_ps, o2t_act, o2t_dve = sem("o2t_ps"), sem("o2t_act"), sem("o2t_dve")
        ff1_ps, ff1_done, ff2_ps = sem("ff1_ps"), sem("ff1_done"), sem("ff2_ps")
        b2_done, beta_done, ffn_done, fin_done = sem("b2_done"), sem("beta_done"), sem("ffn_done"), sem("fin_done")
        held = {e: sem(f"held_{e}") for e in ("pool", "dve")}

        def hold(eng, name, s, value):
            eng.wait_ge(s, value)
            eng.sem_inc(held[name], 1)

        def segment(eng, b, layer, quad, hooks=None):
            g0 = b * QB + (0 if layer == 1 else QUADS[1])
            nq = QUADS[layer]
            lo, hi = 2, nq - 2
            hooks = hooks or {}

            def static(q):
                for u in range(4):
                    quad(g0 + q, q, False, u)
                    for step in hooks.get((q, u), ()):
                        step()

            for q in range(-2, min(lo, nq + 2)):
                static(q)
            if hi > lo:
                with eng.Fori(lo, hi) as l:
                    for u in range(4):
                        quad(g0 + l, l, True, u)
            for q in range(max(lo, hi), nq + 2):
                static(q)

        def batches(eng, body):
            body(0, False, True)
            with eng.Fori(1, B - 1) as b:
                body(b, True, True)
            body(B - 1, True, False)

        def live(layer, l, full, d, u=0):
            return full or 0 <= 4 * l + u + d < 4 * QUADS[layer]

        def cols(l, width, size, offset=0):
            return bass.ds(l * width + offset, size)

        def tokens(dram, b):
            return dram[bass.ds(b, 1), :, :].rearrange("b (t p) f -> p (b t) f", p=P)

        block = ctx.enter_context(nc.Block())

        @block.sync
        def _(sp):
            def load(to, src, b, s):
                sp.dma_start(to[:, :, :], tokens(src, b)).then_inc(s, DMA)

            def turn(s, has_prev, has_next):
                sp.wait_ge(x1_done, s * 3 + 3)
                sp.dma_start(tokens(x1_dram, s), xx[:, :, :]).then_inc(x1_saved, DMA)
                sp.wait_ge(yn_done[LN_X1], s + 1)
                sp.wait_ge(x1_saved, s * DMA + DMA)
                if has_prev:
                    load(xx, x1_dram, s - 1, x1_back)
                    sp.wait_ge(fin_done, s)
                    sp.dma_start(tokens(out, s - 1), yy[:, :, :]).then_inc(out_done, DMA)
                if has_next:
                    load(xx, x, s + 1, x_in)

            sp.sem_inc(out_done, DMA)
            load(xx, x, 0, x_in)
            batches(sp, turn)
            load(xx, x1_dram, B - 1, x1_back)
            sp.wait_ge(fin_done, B)
            sp.dma_start(tokens(out, B - 1), yy[:, :, :]).then_inc(out_done, DMA)
            sp.wait_ge(out_done, (B + 1) * DMA)

        @block.gpsimd
        def _(pool):
            nc.gpsimd.memset(val_hi[:, :, :, F:V], 1.0)
            nc.gpsimd.memset(valo_hi[:, :].rearrange("p (t v) -> p t v", t=T)[:, :, F:V], 1.0).then_inc(ones_done, 1)
            pool.sem_inc(z_done, X_SLOTS)

            def rsqrt(i, s):
                hold(pool, "pool", mv_done[i], s + 1)
                nc.gpsimd.tensor_scalar(rstd[:, :], mv[:, :, 1], LN_EPS, None, ALU.add).then_inc(eps_done[i], 1)
                pool.wait_ge(eps_done[i], s + 1)
                nc.gpsimd.tensor_tensor(rstd[:, :], rstd[:, :], half_neg[:, :], ALU.pow).then_inc(pow_done[i], 1)
                if i != LN_Y:
                    hold(pool, "pool", pow_done[i], s + 1)
                    nc.gpsimd.tensor_scalar(rstd[:, :], rstd[:, :], LN_SCALE, None, ALU.mult).then_inc(rstd_done[i], 1)

            def add_b2(p, i):
                pool.wait_ge(o2t_ps, p * 2 + 2)
                nc.gpsimd.tensor_tensor(o2t[i], o2t[i], b2_bc[:, :].unsqueeze(1).to_broadcast([P, T // 2, F]), ALU.add).then_inc(b2_done, 1)

            def add_beta(p):
                pool.wait_ge(x1_back, p * DMA + DMA)
                nc.gpsimd.tensor_tensor(xx[:, :, :], xx[:, :, :], beta_bc[:, :].unsqueeze(1).to_broadcast([P, T, F]), ALU.add).then_inc(beta_done, 1)

            def body(b, has_prev, has_next):
                for jt in range(T):
                    pool.wait_ge(f2c_done, b * 2 * T + jt + 1)
                    if jt:
                        pool.wait_ge(bc_ps, b * 2 * T + jt)
                    nc.gpsimd.tensor_tensor(diag[:, :, :], ident[:, :].unsqueeze(1).to_broadcast([P, H, P]),
                                            f2c[:, :].unsqueeze(2).to_broadcast([P, H, P]), ALU.mult).then_inc(diag_done, 1)
                if has_prev:
                    add_b2(b - 1, 0)
                    add_b2(b - 1, 1)
                    add_beta(b - 1)
                hooks = {1: {}, 2: {}}
                if has_prev:
                    hooks[1][(1, 1)] = [lambda: rsqrt(LN_Y, b - 1)]
                if has_next:
                    hooks[1][(6, 2)] = [lambda: rsqrt(LN_X, b + 1)]
                    hooks[2][(0, 3)] = [lambda: rsqrt(LN_X1, b + 1)]
                for layer in (1, 2):
                    def quad(g, l, full, u, layer=layer):
                        n = g * 4
                        if live(layer, l, full, 2, u):
                            pool.wait_ge(r_done, n + u + 3)
                            nc.gpsimd.tensor_tensor(rr[:, u % PAIR, :], rr[:, u % PAIR, :], xr[:, (u + 2) % X_SLOTS, :],
                                                    ALU.add).then_inc(z_done, 1)
                    segment(pool, b, layer, quad, hooks[layer])

            rsqrt(LN_X, 0)
            rsqrt(LN_X1, 0)
            batches(pool, body)
            add_b2(B - 1, 0)
            add_b2(B - 1, 1)
            add_beta(B - 1)
            rsqrt(LN_Y, B - 1)

        @block.scalar
        def _(act):
            def h0(s):
                act.wait_ge(yn_done[LN_X], s + 1)
                nc.scalar.activation(hs_hi[:, :], yy[:, :, :].rearrange("p t f -> p (t f)"), ACT.Relu).then_inc(h0hi_done, 1)

            def z_out(s, k):
                act.wait_ge(z_ps, s * 4 + 2 * k + 1)
                nc.scalar.activation(cat[:, KF + k, :], psum[2 * k][:, :], ACT.Copy, scale=1.0 / LN_SCALE).then_inc(cat_act, 1)

            def h1(s, k):
                act.wait_ge(h1_ps, s * 2 + k + 1)
                nc.scalar.activation(h1_hi[:, k, :], psD[:, :], ACT.Relu).then_inc(h1hi_done, 1)

            def o2_out(p):
                act.wait_ge(o2t_ps, p * 2 + 1)
                nc.scalar.activation(o2T[:, 0, :], psD[:, :], ACT.Copy).then_inc(o2t_act, 1)

            def hidden(p, k):
                act.wait_ge(ff1_ps, p * 2 + k + 1)
                nc.scalar.activation(ffT[k], psum[3 - k][:, :], ACT.Relu, bias=b1_col[:, k:k + 1]).then_inc(ff1_done, 1)

            def body(b, has_prev, has_next):
                for jt in range(T + 1):
                    if jt < T:
                        act.wait_ge(wh_ps, b * T + jt + 1)
                        nc.scalar.activation(val_hi[:, jt, :, 0:F], psum[jt % 2][:, :].rearrange("p (h f) -> p h f", h=H),
                                             ACT.Copy, scale=VAL_SCALE).then_inc(whhi_done, 1)
                    if jt >= 1:
                        act.wait_ge(bc_ps, b * 2 * T + jt)
                        nc.scalar.activation(cat[:, :, (jt - 1) * P:jt * P], psC[:, 512:1024].rearrange("p (h n) -> p h n", h=H),
                                             ACT.Copy).then_inc(f2_ready, 1)
                    if has_prev and jt == 6:
                        o2_out(b - 1)
                hooks = {1: {}, 2: {}}
                if has_prev:
                    hooks[1][(-2, 3)] = [lambda: hidden(b - 1, 0)]
                    hooks[1][(-1, 3)] = [lambda: hidden(b - 1, 1)]
                if has_next:
                    hooks[1][(7, 1)] = [lambda: h0(b + 1)]
                    hooks[1][(8, 2)] = [lambda: z_out(b + 1, 0)]
                    hooks[1][(9, 1)] = [lambda: z_out(b + 1, 1)]
                    hooks[2][(1, 3)] = [lambda: h1(b + 1, 0)]
                    hooks[2][(2, 1)] = [lambda: h1(b + 1, 1)]
                for layer in (1, 2):
                    def quad(g, l, full, u, layer=layer):
                        n = g * 4
                        s0 = 0 if layer == 1 else 4 * T

                        def rectify():
                            if live(layer, l, full, 2, u):
                                m, dq = (u + 2) % 4, (u + 2) // 4
                                act.wait_ge(x_done, n + u + 4)
                                f1 = f1h if layer == 1 else f1o
                                act.wait_ge(p_done, n + u + 1 + PAIR)
                                nc.scalar.activation(rr[:, m % PAIR, :], xr[:, m, :], ACT.Relu, bias=f1[:, cols(l + dq, 4, 1, m)],
                                                     scale=RATIO).then_inc(r_done, 1)

                        post = layer == 1 and live(layer, l, full, -8)
                        if u == 0 and post:
                            act.wait_ge(ht_ps, b * T + l)
                            act.wait_ge(proj_ps, b * T + l - 1)
                            nc.scalar.activation(ht_hi, psD[:, :], ACT.Copy, scale=scale(S_H)).then_inc(hthi_done, 1)
                        if u == 3 and post:
                            act.wait_ge(bc_ps, b * 2 * T + T + l - 1)
                            nc.scalar.activation(f2o[:, cols(l - 2, P, P)], psD[:, 512:512 + P], ACT.Copy).then_inc(f2_ready, 1)
                        rectify()
                        if live(layer, l, full, 0, u):
                            act.wait_ge(pt_ps, n + u + 1)
                            act.wait_ge(mm_done, n + u + 1)
                            nc.scalar.activation(pt_hi[:, u % PAIR, :], psum[u % PAIR][:, :], ACT.Copy).then_inc(hi_done, 1)
                        if live(layer, l, full, 1, u):
                            m, dq = (u + 1) % 4, (u + 1) // 4
                            if m == 0:
                                act.wait_ge(bias_done, g + 3)
                            act.wait_ge(z_done, n + u + 2 + X_SLOTS)
                            nc.scalar.activation(pr[:, m % PAIR, :], rr[:, m % PAIR, :], ACT.Exp, bias=shift[:, cols(l + dq, 4, 1, s0 + m)],
                                                 scale=UNIT).then_inc(p_done, 1)
                        if u < 2 and live(layer, l, full, -4):
                            act.wait_ge(y_done, n + u * PAIR)
                            if u == 0:
                                act.wait_ge(ht_ps, b * T + l if layer == 1 else b * T + T + 1)
                            nc.scalar.activation(eq[:, u * 2 * F:(u + 1) * 2 * F], yq[:, u * 2 * F:(u + 1) * 2 * F], ACT.Exp).then_inc(exp_done, 1)
                        if u == 1 and post:
                            act.wait_ge(proj_ps, b * T + l)
                            nc.scalar.activation(valo_hi[:, cols(l - 2, V, F)], psD[:, 0:F], ACT.Copy, scale=VALO_SCALE).then_inc(valohi_done, 1)
                    segment(act, b, layer, quad, hooks[layer])

            act.sem_inc(p_done, PAIR)
            act.wait_ge(ones_done, 1)
            h0(0)
            z_out(0, 0)
            z_out(0, 1)
            h1(0, 0)
            h1(0, 1)
            batches(act, body)
            act.wait_ge(out_done, B * DMA)
            o2_out(B - 1)
            hidden(B - 1, 0)
            hidden(B - 1, 1)

        @block.vector
        def _(dve):
            half = T // 2

            def stats_of(i, src, t0):
                for t in range(t0, t0 + half):
                    last = nc.vector.bn_stats(stats[:, t, :], src(t))
                if t0:
                    last.then_inc(stats_done[i], 1)

            def means_of(i, s):
                hold(dve, "dve", stats_done[i], s + 1)
                for t in range(T):
                    last = nc.vector.bn_aggr(mv[:, t, :], stats[:, t, :])
                last.then_inc(mv_done[i], 1)

            def normalise(i, s, t0):
                dve.wait_ge(mv_done[i], s + 1)
                dve.wait_ge(rstd_done[i], s + 1)
                if i == LN_X:
                    dve.wait_ge(out_done, out_gone(s))
                for t in range(t0, t0 + half):
                    last = nc.vector.tensor_scalar(yy[:, t, :], xx[:, t, :], mv[:, t, 0:1], rstd[:, t:t + 1], ALU.subtract, ALU.mult)
                if t0:
                    last.then_inc(yn_done[i], 1)

            def out_gone(s):
                return DMA if isinstance(s, int) and s < 2 else s * DMA

            def h0(s):
                dve.wait_ge(yn_done[LN_X], s + 1)
                dve.wait_ge(h0hi_done, s + 1)
                nc.vector.scalar_tensor_tensor(hs_lo[:, :], yy[:, :, :].rearrange("p t f -> p (t f)"), 0.0, hs_hi[:, :],
                                               ALU.max, ALU.subtract).then_inc(h0_done, 1)

            def add_bias():
                for t in range(T):
                    last = nc.vector.scalar_tensor_tensor(xx[:, t, :], b0_bc[:, :], deg[:, t:t + 1], xx[:, t, :], ALU.mult, ALU.add)
                last.then_inc(x1_done, 1)

            def d_out(s, k):
                dve.wait_ge(z_ps, s * 4 + 2 * k + 2)
                nc.vector.tensor_scalar(cat[:, k, :], psB[:, :], 1.0 / LN_SCALE, None, ALU.mult).then_inc(cat_dve, 1)

            def x1(s, i):
                dve.wait_ge(x1_done, s * 3 + 1)
                dve.wait_ge(x1_ps, s * 2 + i + 1)
                to = xx[:, i * half:(i + 1) * half, :]
                nc.vector.tensor_tensor(to, psum[i][:, :].rearrange("p (t f) -> p t f", f=F), to, ALU.add).then_inc(x1_done, 1)

            def stats_x1(s, t0):
                hold(dve, "dve", x1_done, s * 3 + 3)
                stats_of(LN_X1, lambda t: xx[:, t, :], t0)

            def stats_x(s, t0):
                hold(dve, "dve", x_in, s * DMA + DMA)
                stats_of(LN_X, lambda t: xx[:, t, :], t0)

            def h1(s, k):
                dve.wait_ge(h1hi_done, s * 2 + k + 1)
                nc.vector.scalar_tensor_tensor(h1_lo[:, k, :], psD[:, :], 0.0, h1_hi[:, k, :], ALU.max, ALU.subtract).then_inc(h1_done, 1)

            def o2_out(p):
                dve.wait_ge(o2t_ps, p * 2 + 2)
                nc.vector.tensor_copy(o2T[:, 1, :], psD[:, :]).then_inc(o2t_dve, 1)

            def ffn(p, i):
                dve.wait_ge(b2_done, p * 2 + i + 1)
                dve.wait_ge(ff2_ps, p * 2 + i + 1)
                nc.vector.tensor_tensor(o2[i], psum[3 - i][:, :], o2[i], ALU.add).then_inc(ffn_done, 1)

            def stats_y(p, i):
                hold(dve, "dve", ffn_done, p * 2 + i + 1)
                stats_of(LN_Y, lambda t: o2t[t // half][:, t % half, :], i * half)

            def gain(p, i):
                dve.wait_ge(mv_done[LN_Y], p + 1)
                for t in range(i * half, (i + 1) * half):
                    last = nc.vector.scalar_tensor_tensor(yy[:, t, :], o2t[i][:, t % half, :], mv[:, t, 0:1], gamma_bc[:, :], ALU.subtract, ALU.mult)
                if i:
                    last.then_inc(yn_done[LN_Y], 1)

            def finish(p, i):
                dve.wait_ge(yn_done[LN_Y], p + 1)
                dve.wait_ge(pow_done[LN_Y], p + 1)
                dve.wait_ge(beta_done, p + 1)
                for t in range(i * half, (i + 1) * half):
                    last = nc.vector.scalar_tensor_tensor(yy[:, t, :], yy[:, t, :], rstd[:, t:t + 1], xx[:, t, :], ALU.mult, ALU.add)
                if i:
                    last.then_inc(fin_done, 1)

            def body(b, has_prev, has_next):
                for jt in range(T):
                    dve.wait_ge(wh_ps, b * T + jt + 1)
                    if jt:
                        dve.wait_ge(diag_done, b * 2 * T + jt)
                    nc.vector.tensor_scalar(f1h[:, jt * H:(jt + 1) * H], psC[:, 0:H], scale(S_F1), None, ALU.mult)
                    nc.vector.tensor_scalar(f2c[:, :], psC[:, H:NF], scale(S_F2), None, ALU.mult).then_inc(f2c_done, 1)
                    dve.wait_ge(whhi_done, b * T + jt + 1)
                    nc.vector.scalar_tensor_tensor(val_lo[:, jt, :, 0:F], psum[jt % 2][:, :].rearrange("p (h f) -> p h f", h=H), VAL_SCALE,
                                                   val_hi[:, jt, :, 0:F], ALU.mult, ALU.subtract).then_inc(wh_done, 1)
                    if has_prev and jt == 7:
                        o2_out(b - 1)
                hooks = {1: {}, 2: {}}
                if has_prev:
                    p = b - 1
                    hooks[1].update({
                        (0, 0): [lambda: ffn(p, 0)], (0, 1): [lambda: ffn(p, 1)], (0, 2): [lambda: stats_y(p, 0)],
                        (0, 3): [lambda: stats_y(p, 1)], (1, 0): [lambda: means_of(LN_Y, p)],
                        (1, 1): [lambda: gain(p, 0)], (1, 2): [lambda: gain(p, 1), lambda: finish(p, 0)], (1, 3): [lambda: finish(p, 1)],
                    })
                if has_next:
                    s = b + 1
                    hooks[1].update({
                        (6, 0): [lambda: stats_x(s, 0)], (6, 1): [lambda: stats_x(s, half), lambda: means_of(LN_X, s)],
                        (6, 3): [lambda: normalise(LN_X, s, 0)], (7, 0): [lambda: normalise(LN_X, s, half)], (7, 2): [lambda: h0(s)],
                        (8, 0): [add_bias], (8, 2): [lambda: d_out(s, 0)], (9, 1): [lambda: d_out(s, 1)],
                    })
                    hooks[2].update({
                        (-1, 2): [lambda: x1(s, 0)], (-1, 3): [lambda: x1(s, 1)], (0, 0): [lambda: stats_x1(s, 0)],
                        (0, 1): [lambda: stats_x1(s, half), lambda: means_of(LN_X1, s)], (0, 3): [lambda: normalise(LN_X1, s, 0)],
                        (1, 0): [lambda: normalise(LN_X1, s, half)], (2, 0): [lambda: h1(s, 0)], (2, 2): [lambda: h1(s, 1)],
                    })
                for layer in (1, 2):
                    def quad(g, l, full, u, layer=layer):
                        n = g * 4
                        s0 = 0 if layer == 1 else 4 * T

                        def masked_row():
                            if not live(layer, l, full, 5, u):
                                return
                            m, dq = (u + 5) % 4, (u + 5) // 4
                            if layer == 1 and m == 0:
                                dve.wait_ge(x_done, n + 8)
                                dve.sem_inc(held["dve"], 1)
                                nc.vector.tensor_copy(mask_row[:, :], mask_add[:, cols(l + 2, N, N)]).then_inc(row_done, 1)
                            hold(dve, "dve", bias_done, g + dq + 1)
                            hold(dve, "dve", z_done, n + u + 6)
                            if layer == 1:
                                if m == 0:
                                    if not full and l == -2:
                                        hold(dve, "dve", f2_ready, b * 2 * T + T)
                                    hold(dve, "dve", row_done, b * T + l + 3)
                                row, f2 = mask_row[:, :], cat[:, m, :]
                            else:
                                if m == 0 and l == -2:
                                    hold(dve, "dve", f2_ready, b * 2 * T + 2 * T)
                                tile = 4 * (l + dq) + m
                                row, f2 = mask_add[:, tile * N:(tile + 1) * N], f2o[:, :]
                            nc.vector.tensor_tensor_reduce(out=xr[:, m, :], in0=f2, in1=row, scale=1.0, scalar=MASKED * 2,
                                                           op0=ALU.add, op1=ALU.max, accum_out=mx[:, m:m + 1]).then_inc(x_done, 1)

                        def maxima():
                            f1 = (f1h if layer == 1 else f1o)[:, cols(l + 1, 4, 4)]
                            dve.wait_ge(x_done, n + 9)
                            nc.vector.scalar_tensor_tensor(zt[:, 0, :], mx[:, :], RATIO, f1, ALU.mult, ALU.add).then_inc(zt_done, 1)
                            dve.wait_ge(zt_done, g * 2 + 3)
                            nc.vector.scalar_tensor_tensor(zt[:, 1, :], zt[:, 0, :], 0.0, mx[:, :], ALU.max, ALU.add).then_inc(zt_done, 1)
                            dve.wait_ge(zt_done, g * 2 + 4)
                            nc.vector.tensor_scalar(shift[:, cols(l + 1, 4, 4, s0)], zt[:, 1, :], -UNIT, None, ALU.mult).then_inc(bias_done, 1)

                        post = layer == 1 and live(layer, l, full, -8)
                        if live(layer, l, full, -1, u):
                            k = (u - 1) % PAIR
                            dve.wait_ge(hi_done, n + u)
                            nc.vector.tensor_tensor(pt_lo[:, k, :], psum[k][:, :], pt_hi[:, k, :], ALU.subtract).then_inc(lo_done, 1)
                        if u == 0 and post:
                            dve.wait_ge(hthi_done, b * T + l - 1)
                            nc.vector.scalar_tensor_tensor(ht_lo, psD[:, :], scale(S_H), ht_hi, ALU.mult, ALU.subtract).then_inc(ht_done, 1)
                        masked_row()
                        if u == 2 and live(layer, l, full, 4):
                            maxima()
                        if live(layer, l, full, -2, u):
                            k = (u - 2) % 4
                            o = psC[:, (k % PAIR) * 512:(k % PAIR) * 512 + F + 1]
                            dve.wait_ge(mm_done, n + u - 1 + PAIR)
                            nc.vector.reciprocal(rden[:, k:k + 1], o[:, F:F + 1]).then_inc(rden_done, 1)
                            dve.wait_ge(rden_done, n + u - 1)
                            nc.vector.tensor_scalar(yq[:, k * F:(k + 1) * F], o[:, 0:F], rden[:, k:k + 1], scale(S_HINV if layer == 1 else S_OINV),
                                                    ALU.mult, ALU.mult).then_inc(y_done, 1)
                        if u in (1, 2) and live(layer, l, full, -4):
                            part = slice((u - 1) * 2 * F, u * 2 * F)
                            dve.wait_ge(exp_done, g * 2 + u - 2)
                            nc.vector.tensor_scalar(eq[:, part], eq[:, part], 1.0, -1.0, ALU.min, ALU.add).then_inc(em1_done, 1)
                            dve.wait_ge(em1_done, g * 2 + u - 2)
                            to = (eq if layer == 1 else o2[l - 1])[:, part]
                            nc.vector.scalar_tensor_tensor(to, yq[:, part], 0.0, eq[:, part], ALU.max, ALU.add).then_inc(elu_done, 1)
                        if u == 1 and post:
                            dve.wait_ge(valohi_done, b * T + l - 1)
                            nc.vector.scalar_tensor_tensor(valo_lo[:, cols(l - 2, V, F)], psD[:, 0:F], VALO_SCALE, valo_hi[:, cols(l - 2, V, F)],
                                                           ALU.mult, ALU.subtract)
                            nc.vector.tensor_scalar(f1o[:, cols(l - 2, 1, 1)], psD[:, F:F + 1], scale(S_FO1), None, ALU.mult)
                            nc.vector.tensor_scalar(f2oc[:, :], psD[:, F + 1:F + 2], scale(S_FO2), None, ALU.mult).then_inc(f2c_done, 1)
                            dve.wait_ge(f2c_done, b * 2 * T + T + l - 1)
                            nc.vector.tensor_scalar(diag[:, 0, :], ident[:, :], f2oc[:, :], None, ALU.mult).then_inc(diag_done, 1)
                    segment(dve, b, layer, quad, hooks[layer])

            dve.sem_inc(lo_done, PAIR)
            dve.sem_inc(y_done, PAIR)
            dve.sem_inc(bias_done, 1)
            dve.sem_inc(x_done, 1)
            stats_x(0, 0)
            stats_x(0, half)
            means_of(LN_X, 0)
            normalise(LN_X, 0, 0)
            normalise(LN_X, 0, half)
            h0(0)
            add_bias()
            d_out(0, 0)
            d_out(0, 1)
            x1(0, 0)
            x1(0, 1)
            stats_x1(0, 0)
            stats_x1(0, half)
            means_of(LN_X1, 0)
            normalise(LN_X1, 0, 0)
            normalise(LN_X1, 0, half)
            h1(0, 0)
            h1(0, 1)
            batches(dve, body)
            dve.wait_ge(out_done, B * DMA)
            o2_out(B - 1)
            ffn(B - 1, 0)
            ffn(B - 1, 1)
            stats_y(B - 1, 0)
            stats_y(B - 1, 1)
            means_of(LN_Y, B - 1)
            gain(B - 1, 0)
            gain(B - 1, 1)
            finish(B - 1, 0)
            finish(B - 1, 1)

        @block.tensor
        def _(pe):
            def product(to, pairs):
                for i, (lhsT, rhs) in enumerate(pairs):
                    last = nc.tensor.matmul(to, lhsT, rhs, start=i == 0, stop=i == len(pairs) - 1)
                return last

            def z(s, k, c):
                if k == 0 and c == 0:
                    pe.wait_ge(h0hi_done, s + 1)
                    pe.wait_ge(h0_done, s + 1)
                last = product(psum[2 * k][:, c * 512:(c + 1) * 512],
                               [(h[:, jt, k * P:(k + 1) * P], adjT[:, jt, c * 512:(c + 1) * 512]) for jt in range(T) for h in (h0_hi, h0_lo)])
                if c == 1:
                    last.then_inc(z_ps, 1)

            def d(s, k):
                if k == 1:
                    pe.wait_ge(cat_dve, s * 2 + 1)
                for t in range(T):
                    last = product(psB[:, t * P:(t + 1) * P], [(h[:, t, k * P:(k + 1) * P], diag_deg[:, t, :]) for h in (h0_hi, h0_lo)])
                last.then_inc(z_ps, 1)

            def x1(s, i, t0, n):
                if i == 0 and t0 == 0:
                    pe.wait_ge(cat_act, s * 2 + 2)
                    pe.wait_ge(cat_dve, s * 2 + 2)
                for t in range(t0, t0 + n):
                    tok = slice((i * 4 + t) * P, (i * 4 + t + 1) * P)
                    last = product(psum[i][:, t * F:(t + 1) * F], [(cat[:, k, tok], w0T[:, k, :]) for k in range(4)])
                if t0 + n == T // 2:
                    last.then_inc(x1_ps, 1)

            def h1(s, k):
                pe.wait_ge(yn_done[LN_X1], s + 1)
                if k == 1:
                    pe.wait_ge(h1_done, s * 2 + 1)
                for t in range(T):
                    last = nc.tensor.transpose(psD[:, t * P:(t + 1) * P], yy[:, t, k * P:(k + 1) * P], ident[:, :])
                last.then_inc(h1_ps, 1)

            def o2_T(p, k):
                pe.wait_ge(elu_done, (p * QB + QB) * 2)
                if k == 1:
                    pe.wait_ge(o2t_act, p + 1)
                for t in range(T):
                    last = nc.tensor.transpose(psD[:, t * P:(t + 1) * P], o2t[t // 4][:, t % 4, k * P:(k + 1) * P], ident[:, :])
                last.then_inc(o2t_ps, 1)

            def ff1(p, m):
                pe.wait_ge(o2t_dve, p + 1)
                for c in range(2):
                    last = product(psum[3 - m][:, c * 512:(c + 1) * 512],
                                   [(w1_sb[:, k, m * P:(m + 1) * P], o2T[:, k, c * 512:(c + 1) * 512]) for k in range(KF)])
                last.then_inc(ff1_ps, 1)

            def ff2(p, i):
                pe.wait_ge(ff1_done, p * 2 + 2)
                for t in range(T // 2):
                    tok = slice((i * 4 + t) * P, (i * 4 + t + 1) * P)
                    last = product(psum[3 - i][:, t * F:(t + 1) * F], [(ffT[k][:, tok], w2_sb[:, k, :]) for k in range(KF)])
                last.then_inc(ff2_ps, 1)

            def body(b, has_prev, has_next):
                pe.wait_ge(h1_done, b * 2 + 2)
                pe.wait_ge(y_done, b * UB + PAIR)
                for jt in range(T + 1):
                    if jt < T:
                        tok = slice(jt * P, (jt + 1) * P)
                        if jt >= 2:
                            pe.wait_ge(wh_done, b * T + jt - 1)
                        three = [(h1_hi, wh_hi), (h1_hi, wh_lo), (h1_lo, wh_hi)]
                        for c in range(2):
                            product(psum[jt % 2][:, c * 512:(c + 1) * 512],
                                    [(h[:, k, tok], w[:, k, c * 512:(c + 1) * 512]) for k in range(KF) for h, w in three])
                        if jt:
                            pe.wait_ge(f2c_done, b * 2 * T + jt)
                        product(psC[:, 0:NF], [(h[:, k, tok], w[:, k, HF:HF + NF]) for k in range(KF) for h, w in three]).then_inc(wh_ps, 1)
                    if jt >= 1:
                        pe.wait_ge(diag_done, b * 2 * T + jt)
                        if jt >= 2:
                            pe.wait_ge(f2_ready, b * 2 * T + jt - 1)
                        nc.tensor.matmul(psC[:, 512:1024], ones[:, :], diag[:, :, :].rearrange("p h n -> p (h n)"),
                                         start=True, stop=True).then_inc(bc_ps, 1)
                    if has_prev and jt in (5, 7):
                        o2_T(b - 1, (jt - 5) // 2)
                hooks = {1: {}, 2: {}}
                if has_prev:
                    p = b - 1
                    hooks[1][(-2, 0)] = [lambda: ff1(p, 0), lambda: pe.wait_ge(f2_ready, b * 2 * T + T), lambda: ff1(p, 1), lambda: ff2(p, 0),
                                         lambda: ff2(p, 1)]
                if has_next:
                    s = b + 1
                    hooks[1].update({
                        (8, 0): [lambda: z(s, 0, 0)], (8, 1): [lambda: z(s, 0, 1), lambda: d(s, 0)], (8, 2): [lambda: None],
                        (8, 3): [lambda: pe.wait_ge(y_done, b * UB + 4 * T + PAIR), lambda: z(s, 1, 0)],
                        (9, 0): [lambda: z(s, 1, 1), lambda: d(s, 1)],
                        (9, 1): [lambda: x1(s, 0, 0, 2)],
                        (9, 3): [lambda: x1(s, 0, 2, 2), lambda: x1(s, 1, 0, 4)],
                    })
                    hooks[2].update({
                        (-1, 3): [lambda: pe.wait_ge(x1_done, s * 3 + 3)],
                        (1, 2): [lambda: h1(s, 0)], (2, 0): [lambda: h1(s, 1)],
                    })
                for layer in (1, 2):
                    def quad(g, l, full, u, layer=layer):
                        n = g * 4
                        if live(layer, l, full, 0, u):
                            pe.wait_ge(p_done, n + u + 1 + PAIR)
                            pe.wait_ge(lo_done, n + u + 1)
                            for t in range(T):
                                last = nc.tensor.transpose(psum[u % PAIR][:, t * P:(t + 1) * P], pr[:, u % PAIR, t * P:(t + 1) * P], ident[:, :])
                            last.then_inc(pt_ps, 1)
                        if live(layer, l, full, -1, u):
                            m = (u - 1) % 4
                            o = psC[:, (m % PAIR) * 512:(m % PAIR) * 512 + 512]
                            hi, lo = pt_hi[:, m % PAIR, :], pt_lo[:, m % PAIR, :]
                            if has_prev and layer == 1 and not full and l == 0 and u == 1:
                                pe.wait_ge(ffn_done, (b - 1) * 2 + 2)
                            pe.wait_ge(y_done, n + u)
                            pe.wait_ge(hi_done, n + u)
                            for t in range(T):
                                vh = val_hi[:, t, m, 0:F + 1] if layer == 1 else valo_hi[:, t * V:t * V + F + 1]
                                vl = val_lo[:, t, m, 0:F] if layer == 1 else valo_lo[:, t * V:t * V + F]
                                nc.tensor.matmul(o[:, 0:F + 1], hi[:, t * P:(t + 1) * P], vh, start=t == 0, stop=False)
                                nc.tensor.matmul(o[:, 0:F], hi[:, t * P:(t + 1) * P], vl, start=False, stop=False)
                            pe.wait_ge(lo_done, n + u + PAIR)
                            for t in range(T):
                                vh = val_hi[:, t, m, 0:F + 1] if layer == 1 else valo_hi[:, t * V:t * V + F + 1]
                                last = nc.tensor.matmul(o[:, 0:F + 1], lo[:, t * P:(t + 1) * P], vh, start=False, stop=t == T - 1)
                            last.then_inc(mm_done, 1)
                        if u == 2 and layer == 1 and live(layer, l, full, -8):
                            pe.wait_ge(diag_done, b * 2 * T + T + l - 1)
                            nc.tensor.matmul(psD[:, 512:512 + P], ones[:, :], diag[:, 0, :], start=True, stop=True).then_inc(bc_ps, 1)
                        if u == 0 and layer == 1 and live(layer, l, full, -8):
                            pe.wait_ge(ht_done, b * T + l - 1)
                            product(psD[:, 0:V], [(h[:, k * P:(k + 1) * P], w[:, k, :]) for k in range(KH)
                                                  for h, w in ((ht_hi, wo_hi), (ht_hi, wo_lo), (ht_lo, wo_hi))]).then_inc(proj_ps, 1)
                        if u == 3 and layer == 1 and live(layer, l, full, -4):
                            pe.wait_ge(elu_done, g * 2)
                            pe.wait_ge(f2_ready, b * 2 * T + T + l - 1)
                            for k in range(KH):
                                last = nc.tensor.transpose(psD[:, k * P:(k + 1) * P], eq[:, k * P:(k + 1) * P], ident[:, :])
                            last.then_inc(ht_ps, 1)
                    segment(pe, b, layer, quad, hooks[layer])

            pe.sem_inc(mm_done, PAIR)
            pe.sem_inc(ht_ps, 1)
            pe.sem_inc(proj_ps, 1)
            for k in range(KF):
                z(0, k, 0)
                z(0, k, 1)
                d(0, k)
            x1(0, 0, 0, 4)
            x1(0, 1, 0, 4)
            h1(0, 0)
            h1(0, 1)
            batches(pe, body)
            o2_T(B - 1, 0)
            o2_T(B - 1, 1)
            ff1(B - 1, 0)
            ff1(B - 1, 1)
            ff2(B - 1, 0)
            ff2(B - 1, 1)


_INS = ['x', 'adj', 'L0_gnn_W', 'L0_gnn_b', 'L1_gnn_W_heads', 'L1_gnn_a_heads', 'L1_gnn_W_out', 'L1_gnn_a_out',
        'L1_gnn_w1', 'L1_gnn_b1', 'L1_gnn_w2', 'L1_gnn_b2', 'L1_gnn_ln_gamma', 'L1_gnn_ln_beta']


def kernel(**inputs):
    import numpy as np
    import concourse.bacc as bacc
    from concourse.bass_utils import run_bass_kernel_spmd

    nc = bacc.Bacc("TRN2", target_bir_lowering=False, num_devices=1)
    arrays, args = {}, []
    for name in _INS:
        a = np.ascontiguousarray(inputs[name])
        arrays[f"in_{name}"] = a
        args.append(nc.dram_tensor(f"in_{name}", a.shape, mybir.dt.from_np(a.dtype), kind="ExternalInput").ap())
    out = nc.dram_tensor("out", arrays["in_x"].shape, F32, kind="ExternalOutput").ap()
    build(nc, *args, out)
    r = run_bass_kernel_spmd(nc, [arrays], core_ids=[0])
    return r.results[0]["out"]
```

```python
from contextlib import ExitStack

import concourse.bass as bass
from concourse import mybir

ALU = mybir.AluOpType
ACT = mybir.ActivationFunctionType
F32, F16, BF16, I32 = mybir.dt.float32, mybir.dt.float16, mybir.dt.bfloat16, mybir.dt.int32
AX = mybir.AxisListType.X

P = 128
LN_EPS = 1e-5
ALPHA = 0.01
UNIT = 2.0 ** -7
LIN = ALPHA / UNIT
STEP = (1.0 - ALPHA) / UNIT
RATIO = (1.0 - ALPHA) / ALPHA
MASKED = -(2.0 ** 100)
LN_LOG = 11
W_LOG = 13
LN_SCALE = 2.0 ** LN_LOG
WH_LOG = 15 - 4
VAL_SCALE = 2.0 ** (WH_LOG - LN_LOG - W_LOG)
CAT_LOG = 1
F2_SCALE = 2.0 ** -13
VALO_SCALE = 2.0 ** (6 - WH_LOG - W_LOG)
X_SLOTS = 4
PAIR = 2


def build(nc, x, adj, w0, b0, w_heads, a_heads, w_out, a_out, w1, b1, w2, b2, gamma, beta, out):
    B, N, F = x.shape
    H = w_heads.shape[0]
    T = N // P
    KF = F // P
    HF = H * F
    KH = HF // P
    V = F + 2
    NF = 2 * H
    assert H == 4 and T == 8 and KF == 2 and HF == N
    QUADS = {1: T, 2: T // 4}
    UB = 4 * (QUADS[1] + QUADS[2])
    QB = QUADS[1] + QUADS[2]
    DMA = 16

    with ExitStack() as ctx:
        def sb(name, shape, dt, stack=ctx):
            return stack.enter_context(nc.sbuf_tensor(name, shape, dt))

        def sem(name):
            return ctx.enter_context(nc.semaphore(name))

        mask_add = sb("mask_add", [P, T * N], BF16)
        adjT = sb("adjT", [P, T, N], F16)
        diag_deg = sb("diag_deg", [P, T, P], F16)
        deg = sb("deg", [P, T], F32)
        w0_hi = sb("w0_hi", [P, 2 * KF, F], F16)
        w0_lo = sb("w0_lo", [P, 2 * KF, F], F16)
        sc0 = sb("sc0", [P, 2], F32)
        wh_hi = sb("wh_hi", [P, KF, HF + NF], F16)
        wh_lo = sb("wh_lo", [P, KF, HF + NF], F16)
        wo_hi = sb("wo_hi", [P, KH, V], F16)
        wo_lo = sb("wo_lo", [P, KH, V], F16)
        w1_sb = sb("w1_sb", [P, KF, F], F32)
        w2_sb = sb("w2_sb", [P, KF, F], F32)
        b1_col = sb("b1_col", [P, KF], F32)
        b0_bc = sb("b0_bc", [P, F], F32)
        b2_bc = sb("b2_bc", [P, F], F32)
        gamma_bc = sb("gamma_bc", [P, F], F32)
        beta_bc = sb("beta_bc", [P, F], F32)
        ident = sb("ident", [P, P], F32)
        ident16 = sb("ident16", [P, P], F16)
        ones = sb("ones", [P, P], F32)
        ones16 = sb("ones16", [P, P], F16)
        half_neg = sb("half_neg", [P, T], F32)
        sc = sb("sc", [P, 16], F32)
        S_WH, S_WO, S_WA, S_WAO, S_F, S_H, S_HINV, S_OINV, S_FO, S_F1, S_FO1, S_FO2, S_ROW = range(13)

        def scale(i):
            return sc[:, i:i + 1]

        psum = [ctx.enter_context(nc.psum_tensor(f"ps{i}", [P, 1024], F32)) for i in range(4)]
        psA, psB, psC, psD = psum

        xx = sb("xx", [P, T, F], F32)
        yy = sb("yy", [P, T, F], F32)
        hs_hi = sb("hs_hi", [P, 2048], F16)
        hs_lo = sb("hs_lo", [P, 2048], F16)
        cat = sb("cat", [P, 4, N], F32)
        stats = sb("stats", [P, T, 6], F32)
        mv = sb("mv", [P, T, 2], F32)
        rstd = sb("rstd", [P, T], F32)
        cat16 = cat[:, :, :].rearrange("p k n -> p (k n)").bitcast(F16).rearrange("p (a k n) -> p a k n", a=2, k=2 * KF)
        h0_hi = hs_hi[:, :].rearrange("p (t f) -> p t f", t=T)
        h0_lo = hs_lo[:, :].rearrange("p (t f) -> p t f", t=T)
        h1_hi = hs_hi[:, :].rearrange("p (k n) -> p k n", k=KF)
        h1_lo = hs_lo[:, :].rearrange("p (k n) -> p k n", k=KF)

        LN_X, LN_X1, LN_Y = "x", "x1", "y"
        stats_done = {i: sem(f"stats_done_{i}") for i in (LN_X, LN_X1, LN_Y)}
        mv_done = {i: sem(f"mv_done_{i}") for i in (LN_X, LN_X1, LN_Y)}
        eps_done = {i: sem(f"eps_done_{i}") for i in (LN_X, LN_X1, LN_Y)}
        pow_done = {i: sem(f"pow_done_{i}") for i in (LN_X, LN_X1, LN_Y)}
        rstd_done = {i: sem(f"rstd_done_{i}") for i in (LN_X, LN_X1)}
        yn_done = {i: sem(f"yn_done_{i}") for i in (LN_X, LN_X1, LN_Y)}
        x_in, x1_saved, x1_back, out_done = sem("x_in"), sem("x1_saved"), sem("x1_back"), sem("out_done")
        h0hi_done, h0_done = sem("h0hi_done"), sem("h0_done")
        z_ps, cat_act, cat_dve = sem("z_ps"), sem("cat_act"), sem("cat_dve")
        x1_ps, x1_done, h1_ps = sem("x1_ps"), sem("x1_done"), sem("h1_ps")
        h1hi_done, h1_done = sem("h1hi_done"), sem("h1_done")
        held = {e: sem(f"held_{e}") for e in ("pool", "dve")}

        def hold(eng, name, s, value):
            eng.wait_ge(s, value)
            eng.sem_inc(held[name], 1)

        def tokens(dram, b):
            return dram[bass.ds(b, 1), :, :].rearrange("b (t p) f -> p (b t) f", p=P)

        half = T // 2

        def gpsimd_stages(pool):
            def rsqrt(i, s):
                hold(pool, "pool", mv_done[i], s + 1)
                nc.gpsimd.tensor_scalar(rstd[:, :], mv[:, :, 1], LN_EPS, None, ALU.add).then_inc(eps_done[i], 1)
                pool.wait_ge(eps_done[i], s + 1)
                nc.gpsimd.tensor_tensor(rstd[:, :], rstd[:, :], half_neg[:, :], ALU.pow).then_inc(pow_done[i], 1)
                if i != LN_Y:
                    hold(pool, "pool", pow_done[i], s + 1)
                    nc.gpsimd.tensor_scalar(rstd[:, :], rstd[:, :], LN_SCALE, None, ALU.mult).then_inc(rstd_done[i], 1)
            return rsqrt

        def scalar_stages(act):
            def h0(s):
                act.wait_ge(yn_done[LN_X], s + 1)
                nc.scalar.activation(hs_hi[:, :], yy[:, :, :].rearrange("p t f -> p (t f)"), ACT.Relu).then_inc(h0hi_done, 1)

            def z_out(s, k):
                act.wait_ge(z_ps, s * 4 + 2 * k + 1)
                nc.scalar.activation(cat16[:, 0, KF + k, :], psum[2 * k][:, :], ACT.Copy, scale=2.0 ** CAT_LOG / LN_SCALE).then_inc(cat_act, 1)
                act.wait_ge(z_ps, s * 4 + 2 * k + 2)
                nc.scalar.activation(cat16[:, 0, k, :], psB[:, :], ACT.Copy, scale=2.0 ** CAT_LOG / LN_SCALE).then_inc(cat_act, 1)

            def h1(s, k):
                act.wait_ge(h1_ps, s * 2 + k + 1)
                nc.scalar.activation(h1_hi[:, k, :], psD[:, :], ACT.Relu).then_inc(h1hi_done, 1)
            return h0, z_out, h1

        def vector_stages(dve):
            def stats_of(i, src, t0):
                for t in range(t0, t0 + half):
                    last = nc.vector.bn_stats(stats[:, t, :], src(t))
                if t0:
                    last.then_inc(stats_done[i], 1)

            def means_of(i, s):
                hold(dve, "dve", stats_done[i], s + 1)
                for t in range(T):
                    last = nc.vector.bn_aggr(mv[:, t, :], stats[:, t, :])
                last.then_inc(mv_done[i], 1)

            def normalise(i, s, t0):
                dve.wait_ge(mv_done[i], s + 1)
                dve.wait_ge(rstd_done[i], s + 1)
                if i == LN_X:
                    dve.wait_ge(out_done, out_gone(s))
                for t in range(t0, t0 + half):
                    last = nc.vector.tensor_scalar(yy[:, t, :], xx[:, t, :], mv[:, t, 0:1], rstd[:, t:t + 1], ALU.subtract, ALU.mult)
                if t0:
                    last.then_inc(yn_done[i], 1)

            def out_gone(s):
                return DMA if isinstance(s, int) and s < 2 else s * DMA

            def h0(s):
                dve.wait_ge(yn_done[LN_X], s + 1)
                dve.wait_ge(h0hi_done, s + 1)
                nc.vector.scalar_tensor_tensor(hs_lo[:, :], yy[:, :, :].rearrange("p t f -> p (t f)"), 0.0, hs_hi[:, :],
                                               ALU.max, ALU.subtract).then_inc(h0_done, 1)

            def add_bias():
                for t in range(T):
                    last = nc.vector.scalar_tensor_tensor(xx[:, t, :], b0_bc[:, :], deg[:, t:t + 1], xx[:, t, :], ALU.mult, ALU.add)
                last.then_inc(x1_done, 1)

            def z_out(s, k):
                for i, (to, bank) in enumerate(((KF + k, psum[2 * k]), (k, psB))):
                    dve.wait_ge(cat_act, s * 4 + 2 * k + i + 1)
                    nc.vector.scalar_tensor_tensor(cat16[:, 1, to, :], bank[:, :], 2.0 ** CAT_LOG / LN_SCALE, cat16[:, 0, to, :],
                                                   ALU.mult, ALU.subtract).then_inc(cat_dve, 1)

            def x1(s, i):
                dve.wait_ge(x1_done, s * 3 + 1)
                dve.wait_ge(x1_ps, s * 2 + i + 1)
                to = xx[:, i * half:(i + 1) * half, :]
                nc.vector.scalar_tensor_tensor(to, psum[i][:, :].rearrange("p (t f) -> p t f", f=F), sc0[:, 1:2], to,
                                               ALU.mult, ALU.add).then_inc(x1_done, 1)

            def stats_x1(s, t0):
                hold(dve, "dve", x1_done, s * 3 + (3 if t0 else 2))
                stats_of(LN_X1, lambda t: xx[:, t, :], t0)

            def stats_x(s, t0):
                hold(dve, "dve", x_in, s * DMA + DMA)
                stats_of(LN_X, lambda t: xx[:, t, :], t0)

            def h1(s, k):
                dve.wait_ge(h1hi_done, s * 2 + k + 1)
                nc.vector.scalar_tensor_tensor(h1_lo[:, k, :], psD[:, :], 0.0, h1_hi[:, k, :], ALU.max, ALU.subtract).then_inc(h1_done, 1)
            return stats_of, means_of, normalise, h0, add_bias, z_out, x1, stats_x1, stats_x, h1

        def tensor_stages(pe):
            def product(to, pairs):
                for i, (lhsT, rhs) in enumerate(pairs):
                    last = nc.tensor.matmul(to, lhsT, rhs, start=i == 0, stop=i == len(pairs) - 1)
                return last

            def z(s, k, c):
                if k == 0 and c == 0:
                    pe.wait_ge(h0hi_done, s + 1)
                    pe.wait_ge(h0_done, s + 1)
                last = product(psum[2 * k][:, c * 512:(c + 1) * 512],
                               [(h[:, jt, k * P:(k + 1) * P], adjT[:, jt, c * 512:(c + 1) * 512]) for jt in range(T) for h in (h0_hi, h0_lo)])
                if c == 1:
                    last.then_inc(z_ps, 1)

            def d(s, k):
                if k == 1:
                    pe.wait_ge(cat_dve, s * 4 + 2)
                for t in range(T):
                    last = product(psB[:, t * P:(t + 1) * P], [(h[:, t, k * P:(k + 1) * P], diag_deg[:, t, :]) for h in (h0_hi, h0_lo)])
                last.then_inc(z_ps, 1)

            def x1(s, i, t0, n):
                if i == 0 and t0 == 0:
                    pe.wait_ge(cat_dve, s * 4 + 4)
                for t in range(t0, t0 + n):
                    tok = slice((i * 4 + t) * P, (i * 4 + t + 1) * P)
                    last = product(psum[i][:, t * F:(t + 1) * F], [(cat16[:, a, k, tok], w[:, k, :]) for k in (2, 0, 3, 1) for a, w in ((0, w0_hi), (0, w0_lo), (1, w0_hi))])
                if t0 + n == T // 2:
                    last.then_inc(x1_ps, 1)

            def h1(s, k):
                pe.wait_ge(yn_done[LN_X1], s + 1)
                if k == 1:
                    pe.wait_ge(h1_done, s * 2 + 1)
                for t in range(T):
                    last = nc.tensor.transpose(psD[:, t * P:(t + 1) * P], yy[:, t, k * P:(k + 1) * P], ident[:, :])
                last.then_inc(h1_ps, 1)
            return product, z, d, x1, h1

        with ExitStack() as tmp:
            adj_i = sb("adj_i", [P, T, N], I32, tmp)
            adj16 = sb("adj16", [P, T, N], F16, tmp)
            w0_sb = sb("w0_sb", [P, KF, 2 * F], F32, tmp)
            whf = sb("whf", [P, KF, H, F], F32, tmp)
            wof = sb("wof", [P, KH, F], F32, tmp)
            ah_bc = sb("ah_bc", [P, H, 2, F], F32, tmp)
            ao_bc = sb("ao_bc", [P, 2, F], F32, tmp)
            waf = sb("waf", [P, KF, 2, H], F32, tmp)
            wao = sb("wao", [P, KH, 2], F32, tmp)
            sq = sb("sq", [P, KF * HF], F32, tmp)
            sqo = sb("sqo", [P, KH * F], F32, tmp)
            sqa = sb("sqa", [P, 32], F32, tmp)
            sq0 = sb("sq0", [P, KF * 2 * F], F32, tmp)
            nsq0 = sb("nsq0", [P, 1], F32, tmp)
            ei0 = sb("ei0", [P, 1], I32, tmp)
            kf0 = sb("kf0", [P, 1], F32, tmp)
            eb0 = sb("eb0", [P, 2], F32, tmp)
            e0 = sb("e0", [P, 2], I32, tmp)
            junk = sb("junk", [P, F], F32, tmp)
            whf_flat = whf[:, :, :, :].rearrange("p k h f -> p (k h f)")
            wof_flat = wof[:, :, :].rearrange("p k f -> p (k f)")
            waf_flat = waf[:, :, :, :].rearrange("p k c h -> p (k c h)")
            wao_flat = wao[:, :, :].rearrange("p k c -> p (k c)")
            nsq = sb("nsq", [P, 4], F32, tmp)
            ei = sb("ei", [P, 4], I32, tmp)
            ki = sb("ki", [P, 4], I32, tmp)
            kf = sb("kf", [P, 4], F32, tmp)
            ksum = sb("ksum", [P, 2], F32, tmp)
            ebits = sb("ebits", [P, 16], F32, tmp)
            eint = sb("eint", [P, 16], I32, tmp)
            adj_in = [sem(f"adj_in_{q}") for q in range(T // 2)]
            w_in, a_in, c_in, w0_in = sem("w_in"), sem("a_in"), sem("c_in"), sem("w0_in")
            zero_done, ident_done = sem("zero_done"), sem("ident_done")
            adj16_done, at_ps, at_act, at_dve = sem("adj16_done"), sem("at_ps"), sem("at_act"), sem("at_dve")
            w0t_ps, w0hi_done, w0_done, diag_deg_done = sem("w0t_ps"), sem("w0hi_done"), sem("w0_done"), sem("diag_deg_done")
            sq0_done, norm0_ps, sc0_done = sem("sq0_done"), sem("norm0_ps"), sem("sc0_done")
            sq_done, sqa_done, norm_ps = sem("sq_done"), sem("sqa_done"), sem("norm_ps")
            setup_dve = sem("setup_dve")

            def at_copy(nc_copy, it, s):
                src = (psB if it % 2 == 0 else psD)[:, 0:N // 2].bitcast(F16).rearrange("p (t i) -> p t i", t=T)
                nc_copy(adjT[:, :, it * P:(it + 1) * P], src).then_inc(s, 1)

            with nc.Block() as block:
                @block.sync
                def _(sp):
                    sp.sem_inc(out_done, DMA)
                    sp.dma_start(xx[:, :, :], tokens(x, 0)).then_inc(x_in, DMA)
                    for q in range(T // 2):
                        sp.dma_start(adj_i[:, 2 * q:2 * q + 2, :], adj[2 * q * P:(2 * q + 2) * P, :].rearrange("(t p) j -> p t j", p=P)).then_inc(adj_in[q], DMA)
                    sp.dma_start(b0_bc[:, :], b0.partition_broadcast(P)).then_inc(c_in, DMA)
                    sp.dma_start(b2_bc[:, :], b2.partition_broadcast(P)).then_inc(c_in, DMA)
                    sp.dma_start(gamma_bc[:, :], gamma.partition_broadcast(P)).then_inc(c_in, DMA)
                    sp.dma_start(beta_bc[:, :], beta.partition_broadcast(P)).then_inc(c_in, DMA)
                    sp.dma_start(b1_col[:, :], b1.rearrange("(k p) -> p k", p=P), allow_slow_non_contiguous=True).then_inc(c_in, DMA)
                    sp.dma_start(w1_sb[:, :, :], w1.rearrange("(k p) n -> p k n", p=P)).then_inc(c_in, DMA)
                    sp.dma_start(w2_sb[:, :, :], w2.rearrange("(k p) n -> p k n", p=P)).then_inc(c_in, DMA)
                    sp.wait_ge(c_in, 7 * DMA)

                @block.gpsimd
                def _(pool):
                    rsqrt = gpsimd_stages(pool)
                    nc.gpsimd.memset(ident[:, :], 0.0).then_inc(zero_done, 1)
                    nc.gpsimd.memset(ident16[:, :], 0.0).then_inc(zero_done, 1)
                    nc.gpsimd.memset(half_neg[:, :], -0.5)
                    nc.gpsimd.memset(ones[:, :], 1.0)
                    nc.gpsimd.memset(ones16[:, :], 1.0)
                    pool.wait_ge(zero_done, 2)
                    for m in (ident, ident16):
                        nc.gpsimd.affine_select(out=m[:, :], in_=m[:, :], compare_op=ALU.not_equal, fill=1.0, base=0,
                                                pattern=[[-1, P]], channel_multiplier=1).then_inc(ident_done, 1)
                    rsqrt(LN_X, 0)
                    pool.wait_ge(adj_in[1], DMA)
                    for k in range(KF):
                        pool.dma_start(whf[:, k, :, :], w_heads[:, k * P:(k + 1) * P, :].rearrange("h p f -> p h f")).then_inc(w_in, DMA)
                    pool.dma_start(w0_sb[:, :, :], w0.rearrange("(k p) n -> p k n", p=P)).then_inc(w0_in, DMA)
                    pool.dma_start(wof[:, :, :], w_out.rearrange("(k p) n -> p k n", p=P)).then_inc(w_in, DMA)
                    pool.dma_start(ah_bc[:, :, :, :].rearrange("p h c f -> p (h c f)"), a_heads.rearrange("h c -> (h c)").partition_broadcast(P)).then_inc(a_in, DMA)
                    pool.dma_start(ao_bc[:, :, :].rearrange("p c f -> p (c f)"), a_out.partition_broadcast(P)).then_inc(a_in, DMA)
                    pool.wait_ge(w0_in, DMA)
                    nc.gpsimd.tensor_tensor(sq0[:, :], w0_sb[:, :, :].rearrange("p k n -> p (k n)"), w0_sb[:, :, :].rearrange("p k n -> p (k n)"),
                                            ALU.mult).then_inc(sq0_done, 1)
                    pool.wait_ge(w_in, 3 * DMA)
                    nc.gpsimd.tensor_tensor(sq[:, :], whf_flat, whf_flat, ALU.mult).then_inc(sq_done, 1)
                    nc.gpsimd.tensor_tensor(sqo[:, :], wof_flat, wof_flat, ALU.mult).then_inc(sq_done, 1)
                    rsqrt(LN_X1, 0)

                @block.scalar
                def _(act):
                    h0, z_out, h1 = scalar_stages(act)
                    def at_out(it):
                        act.wait_ge(at_ps, it + 1)
                        at_copy(lambda to, src: nc.scalar.activation(to, src, ACT.Copy), it, at_act)

                    for it in range(T):
                        act.wait_ge(adj_in[it // 2], DMA)
                        nc.scalar.activation(adj16[:, it, :], adj_i[:, it, :], ACT.Copy, accum_out=deg[:, it:it + 1]).then_inc(adj16_done, 1)
                        if it in (3, 5):
                            at_out(it - 3)
                        if it == 5:
                            h0(0)
                    at_out(4)
                    at_out(6)
                    act.wait_ge(w0t_ps, 1)
                    act.wait_ge(sc0_done, 1)
                    nc.scalar.activation(w0_hi[:, :, :].rearrange("p k n -> p (k n)"), psC[:, :], ACT.Copy, scale=sc0[:, 0:1]).then_inc(w0hi_done, 1)
                    z_out(0, 0)
                    z_out(0, 1)
                    h1(0, 0)
                    h1(0, 1)

                @block.vector
                def _(dve):
                    stats_of, means_of, normalise, h0, add_bias, z_out, x1, stats_x1, stats_x, h1 = vector_stages(dve)
                    chain = [0]

                    def link(instruction):
                        chain[0] += 1
                        instruction.then_inc(setup_dve, 1)
                        dve.wait_ge(setup_dve, chain[0])

                    def fold(to, w, a):
                        link(nc.vector.tensor_tensor_reduce(out=junk[:, :], in0=w, in1=a, scale=1.0, scalar=0.0, op0=ALU.mult, op1=ALU.add, accum_out=to))

                    def fold_heads(c):
                        for k in range(KF):
                            for h in range(H):
                                fold(waf[:, k, c, h:h + 1], whf[:, k, h, :], ah_bc[:, h, c, :])

                    def fold_out(c):
                        for k in range(KH):
                            fold(wao[:, k, c:c + 1], wof[:, k, :], ao_bc[:, c, :])

                    def split(src, hi, lo, s):
                        link(nc.vector.tensor_scalar(hi, src, scale(s), None, ALU.mult))
                        link(nc.vector.scalar_tensor_tensor(lo, src, scale(s), hi, ALU.mult, ALU.subtract))

                    stats_x(0, 0)
                    stats_x(0, half)
                    means_of(LN_X, 0)
                    normalise(LN_X, 0, 0)
                    normalise(LN_X, 0, half)
                    for it in range(1, T, 2):
                        if it == 5:
                            h0(0)
                        dve.wait_ge(at_ps, it + 1)
                        at_copy(nc.vector.tensor_copy, it, at_dve)
                    dve.wait_ge(norm0_ps, 1)
                    link(nc.vector.reduce_max(nsq0[:, :], psD[:, 512:1024], axis=AX))
                    link(nc.vector.tensor_scalar(ei0[:, :], nsq0[:, :].bitcast(I32), 23, None, ALU.logical_shift_right))
                    link(nc.vector.tensor_scalar(ei0[:, :], ei0[:, :], 129.0, None, ALU.add))
                    link(nc.vector.tensor_scalar(ei0[:, :], ei0[:, :], 1, None, ALU.logical_shift_right))
                    link(nc.vector.tensor_copy(kf0[:, :], ei0[:, :]))
                    nc.vector.tensor_scalar(eb0[:, 0:1], kf0[:, :], -1.0, 254.0 + W_LOG, ALU.mult, ALU.add)
                    link(nc.vector.tensor_scalar(eb0[:, 1:2], kf0[:, :], -float(W_LOG + CAT_LOG), None, ALU.add))
                    link(nc.vector.tensor_scalar(e0[:, :], eb0[:, :], 1.0, 254.0, ALU.max, ALU.min))
                    nc.vector.tensor_scalar(sc0[:, :].bitcast(I32), e0[:, :], 23, None, ALU.logical_shift_left).then_inc(sc0_done, 1)
                    dve.wait_ge(w0hi_done, 1)
                    nc.vector.scalar_tensor_tensor(w0_lo[:, :, :].rearrange("p k n -> p (k n)"), psC[:, :], sc0[:, 0:1],
                                                   w0_hi[:, :, :].rearrange("p k n -> p (k n)"), ALU.mult, ALU.subtract).then_inc(w0_done, 1)
                    dve.wait_ge(ident_done, 2)
                    dve.wait_ge(adj16_done, T)
                    for t in range(T):
                        last = nc.vector.tensor_scalar(diag_deg[:, t, :], ident16[:, :], deg[:, t:t + 1], None, ALU.mult)
                    last.then_inc(diag_deg_done, 1)
                    nc.vector.tensor_scalar(mask_add[:, :], adj16[:, :, :].rearrange("p t j -> p (t j)"), 0.0, MASKED, ALU.is_le, ALU.mult)
                    z_out(0, 0)
                    dve.wait_ge(c_in, 7 * DMA)
                    dve.wait_ge(x_in, DMA)
                    dve.wait_ge(yn_done[LN_X], 1)
                    add_bias()
                    dve.wait_ge(w_in, 3 * DMA)
                    dve.wait_ge(a_in, 2 * DMA)
                    fold_heads(0)
                    z_out(0, 1)
                    fold_heads(1)
                    fold_out(0)
                    fold_out(1)
                    nc.vector.tensor_tensor(sqa[:, 0:16], waf_flat, waf_flat, ALU.mult)
                    nc.vector.tensor_tensor(sqa[:, 16:32], wao_flat, wao_flat, ALU.mult).then_inc(sqa_done, 1)
                    x1(0, 0)
                    stats_x1(0, 0)
                    x1(0, 1)
                    stats_x1(0, half)
                    means_of(LN_X1, 0)
                    dve.wait_ge(norm_ps, 1)
                    nc.vector.reduce_max(nsq[:, 0:1], psC[:, :], axis=AX)
                    nc.vector.reduce_max(nsq[:, 1:2], psD[:, 0:F], axis=AX)
                    nc.vector.reduce_max(nsq[:, 2:3], psD[:, 512:512 + NF], axis=AX)
                    link(nc.vector.reduce_max(nsq[:, 3:4], psD[:, 512 + NF:512 + NF + 2], axis=AX))
                    link(nc.vector.tensor_scalar(ei[:, :], nsq[:, :].bitcast(I32), 23, None, ALU.logical_shift_right))
                    link(nc.vector.tensor_scalar(ei[:, :], ei[:, :], 129.0, None, ALU.add))
                    link(nc.vector.tensor_scalar(ki[:, :], ei[:, :], 1, None, ALU.logical_shift_right))
                    link(nc.vector.tensor_copy(kf[:, :], ki[:, :]))
                    nc.vector.tensor_tensor(ksum[:, 0:1], kf[:, 0:1], kf[:, 1:2], ALU.add)
                    link(nc.vector.tensor_tensor(ksum[:, 1:2], kf[:, 0:1], kf[:, 3:4], ALU.add))
                    link(nc.vector.memset(ebits[:, :], 127.0))
                    nc.vector.tensor_scalar(ebits[:, 0:4], kf[:, 0:4], -1.0, 254.0 + W_LOG, ALU.mult, ALU.add)
                    nc.vector.tensor_scalar(ebits[:, S_F:S_F + 1], kf[:, 2:3], -float(LN_LOG + W_LOG), None, ALU.add)
                    nc.vector.tensor_scalar(ebits[:, S_H:S_H + 1], kf[:, 0:1], -1.0, 254.0 + WH_LOG, ALU.mult, ALU.add)
                    nc.vector.tensor_scalar(ebits[:, S_HINV:S_HINV + 1], kf[:, 0:1], -float(WH_LOG), None, ALU.add)
                    nc.vector.tensor_scalar(ebits[:, S_OINV:S_OINV + 1], ksum[:, 0:1], -127.0 - 6.0, None, ALU.add)
                    link(nc.vector.tensor_scalar(ebits[:, S_FO:S_FO + 1], ksum[:, 1:2], -127.0 - float(WH_LOG + W_LOG), None, ALU.add))
                    link(nc.vector.tensor_scalar(eint[:, :], ebits[:, :], 1.0, 254.0, ALU.max, ALU.min))
                    link(nc.vector.tensor_scalar(sc[:, :].bitcast(I32), eint[:, :], 23, None, ALU.logical_shift_left))
                    nc.vector.tensor_scalar(scale(S_F1), scale(S_F), STEP, None, ALU.mult)
                    nc.vector.tensor_scalar(scale(S_ROW), scale(S_F), LIN / F2_SCALE, None, ALU.mult)
                    nc.vector.tensor_scalar(scale(S_FO1), scale(S_FO), STEP, None, ALU.mult)
                    nc.vector.tensor_scalar(scale(S_FO2), scale(S_FO), LIN, None, ALU.mult)
                    normalise(LN_X1, 0, 0)
                    normalise(LN_X1, 0, half)
                    split(whf[:, :, :, :].rearrange("p k h f -> p k (h f)"), wh_hi[:, :, 0:HF], wh_lo[:, :, 0:HF], S_WH)
                    split(waf[:, :, :, :].rearrange("p k c h -> p k (c h)"), wh_hi[:, :, HF:HF + NF], wh_lo[:, :, HF:HF + NF], S_WA)
                    h1(0, 0)
                    split(wof[:, :, :], wo_hi[:, :, 0:F], wo_lo[:, :, 0:F], S_WO)
                    split(wao[:, :, :], wo_hi[:, :, F:V], wo_lo[:, :, F:V], S_WAO)
                    h1(0, 1)

                @block.tensor
                def _(pe):
                    product, z, d, x1, h1 = tensor_stages(pe)
                    pe.wait_ge(ident_done, 2)
                    for it in range(T):
                        pe.wait_ge(adj16_done, it + 1)
                        if it >= 2:
                            pe.wait_ge((at_act, at_dve)[it % 2], it // 2)
                        for jt in range(T):
                            last = nc.tensor.transpose((psB if it % 2 == 0 else psD)[:, jt * P // 2:(jt + 1) * P // 2].bitcast(F16),
                                                       adj16[:, it, jt * P:(jt + 1) * P], ident16[:, :])
                        last.then_inc(at_ps, 1)
                    pe.wait_ge(w0_in, DMA)
                    for k in range(2 * KF):
                        for o in range(KF):
                            last = nc.tensor.transpose(psC[:, k * F + o * P:k * F + (o + 1) * P], w0_sb[:, o, k * P:(k + 1) * P], ident[:, :])
                    last.then_inc(w0t_ps, 1)
                    pe.wait_ge(sq0_done, 1)
                    pe.wait_ge(at_dve, T // 2)
                    product(psD[:, 512:1024], [(ones[:, :], sq0[:, k * 2 * F:(k + 1) * 2 * F]) for k in range(KF)]).then_inc(norm0_ps, 1)
                    pe.wait_ge(at_act, T // 2)
                    z(0, 0, 0)
                    z(0, 0, 1)
                    pe.wait_ge(diag_deg_done, 1)
                    d(0, 0)
                    pe.wait_ge(w0_done, 1)
                    z(0, 1, 0)
                    z(0, 1, 1)
                    d(0, 1)
                    pe.wait_ge(sq_done, 2)
                    product(psD[:, 0:F], [(ones[:, :], sqo[:, k * F:(k + 1) * F]) for k in range(KH)])
                    x1(0, 0, 0, 4)
                    for c in range(2):
                        product(psC[:, c * 512:(c + 1) * 512], [(ones[:, :], sq[:, k * HF + c * 512:k * HF + (c + 1) * 512]) for k in range(KF)])
                    x1(0, 1, 0, 4)
                    pe.wait_ge(sqa_done, 1)
                    product(psD[:, 512:512 + NF], [(ones[:, :], sqa[:, k * NF:(k + 1) * NF]) for k in range(KF)])
                    product(psD[:, 512 + NF:512 + NF + 2], [(ones[:, :], sqa[:, 16 + 2 * k:18 + 2 * k]) for k in range(KH)]).then_inc(norm_ps, 1)
                    h1(0, 0)
                    h1(0, 1)

        val_hi = sb("val_hi", [P, T, H, V], F16)
        val_lo = sb("val_lo", [P, T, H, V], F16)
        valo_hi = sb("valo_hi", [P, T * V], F16)
        valo_lo = sb("valo_lo", [P, T * V], F16)
        f2o = sb("f2o", [P, N], F32)
        f1h = sb("f1h", [P, T * H], F32)
        f1o = sb("f1o", [P, T], F32)
        f2c = sb("f2c", [P, 2, T * H], F16)
        f2oc = sb("f2oc", [P, 1], F32)
        shift = sb("shift", [P, (T + 2) * 4], F32)
        mx = sb("mx", [P, 4], F32)
        zt = sb("zt", [P, 2, 4], F32)
        rden = sb("rden", [P, 4], F32)
        mask_row = sb("mask_row", [P, N], BF16)
        xr = sb("xr", [P, X_SLOTS, N], F32)
        rr = sb("rr", [P, PAIR, N], F32)
        pr = sb("pr", [P, PAIR, N], F32)
        pt_hi = sb("pt_hi", [P, PAIR, N], F16)
        pt_lo = sb("pt_lo", [P, PAIR, N], F16)
        yq = sb("yq", [P, 4 * F], F32)
        eq = sb("eq", [P, 4 * F], F32)
        ht = sb("ht", [P, 2 * KH * P], F16)
        ht_hi, ht_lo = ht[:, 0:KH * P], ht[:, KH * P:2 * KH * P]
        diag = sb("diag", [P, 2, H * P], F16)
        diag_o = sb("diag_o", [P, P], F32)
        o2 = [ht[:, :].bitcast(F32), f2o[:, :]]
        o2t = [o.rearrange("p (t f) -> p t f", f=F) for o in o2]
        o2T = yy[:, :, :].rearrange("p t f -> p (t f)").rearrange("p (k n) -> p k n", k=KF)
        ffT = [eq[:, :], yq[:, :]]
        x1_dram = nc.dram_tensor("x1_rows", [B, N, F], F32).ap()

        ones_done = sem("ones_done")
        f_ps, f2hi_done, diaglo_done = sem("f_ps"), sem("f2hi_done"), sem("diaglo_done")
        wh_ps, whhi_done, wh_done = sem("wh_ps"), sem("whhi_done"), sem("wh_done")
        f2c_done, diag_done, bc_ps, f2_ready = sem("f2c_done"), sem("diag_done"), sem("bc_ps"), sem("f2_ready")
        row_done, x_done, zt_done, bias_done = sem("row_done"), sem("x_done"), sem("zt_done"), sem("bias_done")
        r_done, z_done, p_done = sem("r_done"), sem("z_done"), sem("p_done")
        pt_ps, hi_done, lo_done, mm_done = sem("pt_ps"), sem("hi_done"), sem("lo_done"), sem("mm_done")
        rden_done, y_done, exp_done = sem("rden_done"), sem("y_done"), sem("exp_done")
        em1_done, elu_done = sem("em1_done"), sem("elu_done")
        ht_ps, hthi_done, ht_done = sem("ht_ps"), sem("hthi_done"), sem("ht_done")
        proj_ps, valohi_done = sem("proj_ps"), sem("valohi_done")
        o2t_ps, o2t_act, o2t_dve = sem("o2t_ps"), sem("o2t_act"), sem("o2t_dve")
        ff1_ps, ff1_done, ff2_ps = sem("ff1_ps"), sem("ff1_done"), sem("ff2_ps")
        gain_done = sem("gain_done")
        b2_done, beta_done, ffn_done, fin_done = sem("b2_done"), sem("beta_done"), sem("ffn_done"), sem("fin_done")
        def segment(eng, b, layer, quad, hooks=None):
            g0 = b * QB + (0 if layer == 1 else QUADS[1])
            nq = QUADS[layer]
            lo, hi = 2, nq - 2
            hooks = hooks or {}

            def static(q):
                for u in range(4):
                    quad(g0 + q, q, False, u)
                    for step in hooks.get((q, u), ()):
                        step()

            for q in range(-2, min(lo, nq + 2)):
                static(q)
            if hi > lo:
                with eng.Fori(lo, hi) as l:
                    for u in range(4):
                        quad(g0 + l, l, True, u)
            for q in range(max(lo, hi), nq + 2):
                static(q)

        def batches(eng, body):
            body(0, False, True)
            with eng.Fori(1, B - 1) as b:
                body(b, True, True)
            body(B - 1, True, False)

        wh_bank = [psum[jt % 2] for jt in range(T - 1)] + [psC]

        last_banks = ((psD, psB), (psA, psC))
        rows_ahead, rows_behind = {2: 0, 3: 1, 4: 2, 5: 4, 6: 6}, {4: 3, 5: 5, 6: 7}

        def wh_steps(tile, row, hooks, i0=0, i1=2 * T):
            for i in range(i0, i1):
                tile(i)
                if i in rows_ahead:
                    row(rows_ahead[i])
                for step in hooks.get(i, ()):
                    step()
                if i in rows_behind:
                    row(rows_behind[i])

        def live(layer, l, full, d, u=0):
            return full or 0 <= 4 * l + u + d < 4 * QUADS[layer]

        def cols(l, width, size, offset=0):
            return bass.ds(l * width + offset, size)

        block = ctx.enter_context(nc.Block())

        @block.sync
        def _(sp):
            def load(to, src, b, s):
                sp.dma_start(to[:, :, :], tokens(src, b)).then_inc(s, DMA)

            def turn(s, has_prev, has_next):
                sp.wait_ge(x1_done, s * 3 + 3)
                sp.dma_start(tokens(x1_dram, s), xx[:, :, :]).then_inc(x1_saved, DMA)
                sp.wait_ge(yn_done[LN_X1], s + 1)
                sp.wait_ge(x1_saved, s * DMA + DMA)
                if has_prev:
                    load(xx, x1_dram, s - 1, x1_back)
                    sp.wait_ge(fin_done, s)
                    sp.dma_start(tokens(out, s - 1), yy[:, :, :]).then_inc(out_done, DMA)
                if has_next:
                    load(xx, x, s + 1, x_in)

            batches(sp, turn)
            load(xx, x1_dram, B - 1, x1_back)
            sp.wait_ge(fin_done, B)
            sp.dma_start(tokens(out, B - 1), yy[:, :, :]).then_inc(out_done, DMA)
            sp.wait_ge(out_done, (B + 1) * DMA)

        @block.gpsimd
        def _(pool):
            rsqrt = gpsimd_stages(pool)
            nc.gpsimd.memset(val_hi[:, :, :, F:V], 1.0)
            nc.gpsimd.memset(valo_hi[:, :].rearrange("p (t v) -> p t v", t=T)[:, :, F:V], 1.0).then_inc(ones_done, 1)
            pool.sem_inc(z_done, X_SLOTS)

            def add_b2(p, i):
                pool.wait_ge(o2t_ps, p * 2 + 2)
                nc.gpsimd.tensor_tensor(o2t[i], o2t[i], b2_bc[:, :].unsqueeze(1).to_broadcast([P, T // 2, F]), ALU.add).then_inc(b2_done, 1)

            def add_beta(p):
                pool.wait_ge(x1_back, p * DMA + DMA)
                nc.gpsimd.tensor_tensor(xx[:, :, :], xx[:, :, :], beta_bc[:, :].unsqueeze(1).to_broadcast([P, T, F]), ALU.add).then_inc(beta_done, 1)

            def gain(p, i):
                pool.wait_ge(yn_done[LN_Y], p * 2 + i // 2 + 1)
                nc.gpsimd.tensor_tensor(yy[:, 2 * i:2 * i + 2, :], yy[:, 2 * i:2 * i + 2, :], gamma_bc[:, :].unsqueeze(1).to_broadcast([P, 2, F]),
                                        ALU.mult).then_inc(gain_done, 1)

            def finish(p, i):
                pool.wait_ge(gain_done, p * 4 + i + 1)
                last = nc.gpsimd.tensor_tensor(yy[:, 2 * i:2 * i + 2, :], yy[:, 2 * i:2 * i + 2, :], xx[:, 2 * i:2 * i + 2, :], ALU.add)
                if i == 3:
                    last.then_inc(fin_done, 1)

            def body(b, has_prev, has_next):
                pool.wait_ge(f2c_done, b * (T + 1) + 1)
                for jt in range(T):
                    if jt:
                        pool.wait_ge(bc_ps, b * 2 * T + jt)
                    nc.gpsimd.tensor_tensor(diag[:, 0, :].rearrange("p (h n) -> p h n", h=H), ident16[:, :].unsqueeze(1).to_broadcast([P, H, P]),
                                            f2c[:, 0, jt * H:(jt + 1) * H].unsqueeze(2).to_broadcast([P, H, P]), ALU.mult).then_inc(diag_done, 1)
                    if has_prev and jt in (3, 5):
                        add_b2(b - 1, (jt - 3) // 2)
                if has_prev:
                    add_beta(b - 1)
                hooks = {1: {}, 2: {}}
                if has_prev:
                    p = b - 1
                    hooks[1].update({
                        (0, 1): [lambda: rsqrt(LN_Y, p)], (1, 0): [lambda: gain(p, 0), lambda: gain(p, 1)],
                        (1, 1): [lambda: gain(p, 2), lambda: gain(p, 3)], (1, 2): [lambda: finish(p, 0), lambda: finish(p, 1)],
                        (1, 3): [lambda: finish(p, 2), lambda: finish(p, 3)],
                    })
                if has_next:
                    hooks[1][(6, 3)] = [lambda: rsqrt(LN_X, b + 1)]
                    hooks[2][(0, 1)] = [lambda: rsqrt(LN_X1, b + 1)]
                for layer in (1, 2):
                    def quad(g, l, full, u, layer=layer):
                        n = g * 4
                        if live(layer, l, full, 2, u):
                            pool.wait_ge(r_done, n + u + 3)
                            nc.gpsimd.tensor_tensor(rr[:, u % PAIR, :], rr[:, u % PAIR, :], xr[:, (u + 2) % X_SLOTS, :],
                                                    ALU.add).then_inc(z_done, 1)
                    segment(pool, b, layer, quad, hooks[layer])

            batches(pool, body)
            add_b2(B - 1, 0)
            add_b2(B - 1, 1)
            add_beta(B - 1)
            rsqrt(LN_Y, B - 1)

        @block.scalar
        def _(act):
            h0, z_out, h1 = scalar_stages(act)

            def o2_out(p, bank=psD):
                act.wait_ge(o2t_ps, p * 2 + 1)
                nc.scalar.activation(o2T[:, 0, :], bank[:, :], ACT.Copy).then_inc(o2t_act, 1)

            def hidden(p, k, bank=psD):
                act.wait_ge(ff1_ps, p * 2 + k + 1)
                nc.scalar.activation(ffT[k], bank[:, :], ACT.Relu, bias=b1_col[:, k:k + 1]).then_inc(ff1_done, 1)

            def body(b, has_prev, has_next):
                def wh(i):
                    if i % 2:
                        act.wait_ge(wh_ps, b * T + i // 2 + 1)
                        nc.scalar.activation(val_hi[:, i // 2, :, 0:F], wh_bank[i // 2][:, :].rearrange("p (h f) -> p h f", h=H),
                                             ACT.Copy, scale=VAL_SCALE).then_inc(whhi_done, 1)

                def row(jt):
                    act.wait_ge(bc_ps, b * 2 * T + jt + 1)
                    nc.scalar.activation(cat[:, :, jt * P:(jt + 1) * P], psC[:, jt % 2 * 512:(jt % 2 + 1) * 512].rearrange("p (h n) -> p h n", h=H),
                                         ACT.Copy, scale=scale(S_ROW)).then_inc(f2_ready, 1)

                wh_steps(wh, row, {1: [lambda: o2_out(b - 1)], 4: [lambda: hidden(b - 1, 0)], 5: [lambda: hidden(b - 1, 1)]} if has_prev else {},
                         0, 8)
                hooks = {1: {(-1, 2): [lambda: wh(9), lambda: wh(11)], (-1, 3): [lambda: wh(13)]}, 2: {}}
                if has_next:
                    hooks[1][(7, 2)] = [lambda: h0(b + 1)]
                    hooks[1][(8, 2)] = [lambda: z_out(b + 1, 0)]
                    hooks[1][(9, 0)] = [lambda: z_out(b + 1, 1)]
                    hooks[2][(1, 1)] = [lambda: h1(b + 1, 0)]
                    hooks[2][(1, 3)] = [lambda: h1(b + 1, 1)]
                for layer in (1, 2):
                    def quad(g, l, full, u, layer=layer):
                        n = g * 4
                        s0 = 0 if layer == 1 else 4 * T

                        def rectify():
                            if live(layer, l, full, 2, u):
                                m, dq = (u + 2) % 4, (u + 2) // 4
                                act.wait_ge(x_done, n + u + 4)
                                f1 = f1h if layer == 1 else f1o
                                act.wait_ge(p_done, n + u + 1 + PAIR)
                                nc.scalar.activation(rr[:, m % PAIR, :], xr[:, m, :], ACT.Relu, bias=f1[:, cols(l + dq, 4, 1, m)],
                                                     scale=RATIO).then_inc(r_done, 1)

                        post = layer == 1 and live(layer, l, full, -8)
                        if u == 0 and post:
                            act.wait_ge(ht_ps, b * T + l)
                            act.wait_ge(proj_ps, b * T + l - 1)
                            nc.scalar.activation(ht_hi, psD[:, :], ACT.Copy, scale=scale(S_H)).then_inc(hthi_done, 1)
                        if u == 3 and post:
                            act.wait_ge(bc_ps, b * 2 * T + T + l - 1)
                            nc.scalar.activation(f2o[:, cols(l - 2, P, P)], psD[:, 512:512 + P], ACT.Copy).then_inc(f2_ready, 1)
                        rectify()
                        def copy_hi():
                            if live(layer, l, full, 0, u):
                                act.wait_ge(pt_ps, n + u + 1)
                                act.wait_ge(mm_done, n + u + 1)
                                nc.scalar.activation(pt_hi[:, u % PAIR, :], psum[u % PAIR][:, :], ACT.Copy).then_inc(hi_done, 1)

                        def softmax():
                            if live(layer, l, full, 1, u):
                                m, dq = (u + 1) % 4, (u + 1) // 4
                                if m == 0:
                                    act.wait_ge(bias_done, g + 3)
                                act.wait_ge(z_done, n + u + 2 + X_SLOTS)
                                nc.scalar.activation(pr[:, m % PAIR, :], rr[:, m % PAIR, :], ACT.Exp, bias=shift[:, cols(l + dq, 4, 1, s0 + m)],
                                                     scale=UNIT).then_inc(p_done, 1)

                        if not full and l == 0 and u == 0:
                            softmax()
                            if layer == 1:
                                wh(2 * T - 1)
                            copy_hi()
                        else:
                            copy_hi()
                            if u == 1 and post:
                                act.wait_ge(proj_ps, b * T + l)
                                nc.scalar.activation(valo_hi[:, cols(l - 2, V, F)], psD[:, 0:F], ACT.Copy, scale=VALO_SCALE).then_inc(valohi_done, 1)
                            softmax()
                        if u < 2 and live(layer, l, full, -4):
                            act.wait_ge(y_done, n + u * PAIR)
                            if u == 0:
                                act.wait_ge(ht_ps, b * T + l if layer == 1 else b * T + T + 1)
                            nc.scalar.activation(eq[:, u * 2 * F:(u + 1) * 2 * F], yq[:, u * 2 * F:(u + 1) * 2 * F], ACT.Exp).then_inc(exp_done, 1)
                    segment(act, b, layer, quad, hooks[layer])

            act.sem_inc(p_done, PAIR)
            act.wait_ge(ones_done, 1)
            batches(act, body)
            act.wait_ge(out_done, B * DMA)
            o2_out(B - 1)
            for i, (bank, bank1) in enumerate(last_banks):
                hidden(B - 1, i, bank1)

        @block.vector
        def _(dve):
            stats_of, means_of, normalise, h0, add_bias, z_out, x1, stats_x1, stats_x, h1 = vector_stages(dve)

            def o2_out(p, bank=psD):
                dve.wait_ge(o2t_ps, p * 2 + 2)
                nc.vector.tensor_copy(o2T[:, 1, :], bank[:, :]).then_inc(o2t_dve, 1)

            def ffn(p, i, bank=psD):
                dve.wait_ge(b2_done, p * 2 + i + 1)
                dve.wait_ge(ff2_ps, p * 2 + i + 1)
                nc.vector.tensor_tensor(o2[i], bank[:, :], o2[i], ALU.add).then_inc(ffn_done, 1)

            def stats_y(p, i):
                hold(dve, "dve", ffn_done, p * 2 + i + 1)
                stats_of(LN_Y, lambda t: o2t[t // half][:, t % half, :], i * half)

            def normalise_y(p, i):
                dve.wait_ge(mv_done[LN_Y], p + 1)
                dve.wait_ge(pow_done[LN_Y], p + 1)
                for t in range(i * half, (i + 1) * half):
                    last = nc.vector.tensor_scalar(yy[:, t, :], o2t[i][:, t % half, :], mv[:, t, 0:1], rstd[:, t:t + 1], ALU.subtract, ALU.mult)
                last.then_inc(yn_done[LN_Y], 1)

            def gain(p, i):
                dve.wait_ge(mv_done[LN_Y], p + 1)
                for t in range(i * half, (i + 1) * half):
                    last = nc.vector.scalar_tensor_tensor(yy[:, t, :], o2t[i][:, t % half, :], mv[:, t, 0:1], gamma_bc[:, :], ALU.subtract, ALU.mult)
                last.then_inc(yn_done[LN_Y], 1)

            def finish(p, i):
                dve.wait_ge(yn_done[LN_Y], p * 2 + i + 1)
                dve.wait_ge(pow_done[LN_Y], p + 1)
                dve.wait_ge(beta_done, p + 1)
                for t in range(i * half, (i + 1) * half):
                    last = nc.vector.scalar_tensor_tensor(yy[:, t, :], yy[:, t, :], rstd[:, t:t + 1], xx[:, t, :], ALU.mult, ALU.add)
                if i:
                    last.then_inc(fin_done, 1)

            def body(b, has_prev, has_next):
                if has_prev:
                    dve.wait_ge(diag_done, b * 2 * T)
                dve.wait_ge(f_ps, b + 1)
                columns = psD[:, 0:T * NF].rearrange("p (t c) -> p t c", c=NF)
                f2_hi, f2_lo = (f2c[:, i, :].rearrange("p (t h) -> p t h", h=H) for i in (0, 1))
                nc.vector.tensor_scalar(f2_hi, columns[:, :, H:NF], F2_SCALE, None, ALU.mult).then_inc(f2hi_done, 1)
                nc.vector.tensor_scalar(f1h[:, :].rearrange("p (t h) -> p t h", h=H), columns[:, :, 0:H], scale(S_F1), None, ALU.mult)
                dve.wait_ge(f2hi_done, b + 1)
                nc.vector.scalar_tensor_tensor(f2_lo, columns[:, :, H:NF], F2_SCALE, f2_hi, ALU.mult, ALU.subtract).then_inc(f2c_done, 1)

                def wh(i):
                    if i % 2:
                        dve.wait_ge(whhi_done, b * T + i // 2 + 1)
                        nc.vector.scalar_tensor_tensor(val_lo[:, i // 2, :, 0:F], wh_bank[i // 2][:, :].rearrange("p (h f) -> p h f", h=H), VAL_SCALE,
                                                       val_hi[:, i // 2, :, 0:F], ALU.mult, ALU.subtract).then_inc(wh_done, 1)

                def row(jt):
                    if jt == 0:
                        dve.wait_ge(f2c_done, b * (T + 1) + 1)
                    else:
                        dve.wait_ge(bc_ps, b * 2 * T + jt)
                    nc.vector.tensor_tensor(diag[:, 1, :].rearrange("p (h n) -> p h n", h=H), ident16[:, :].unsqueeze(1).to_broadcast([P, H, P]),
                                            f2c[:, 1, jt * H:(jt + 1) * H].unsqueeze(2).to_broadcast([P, H, P]), ALU.mult).then_inc(diaglo_done, 1)

                row(0)
                wh(1)
                row(1)
                row(2)
                wh(3)
                if has_prev:
                    o2_out(b - 1)
                row(3)
                row(4)
                wh(5)
                row(5)
                row(6)
                row(7)
                if has_prev:
                    ffn(b - 1, 0)
                hooks = {1: {(-2, 3): [lambda: wh(7)], (-1, 1): [lambda: wh(9)], (-1, 2): [lambda: wh(11), lambda: wh(13), lambda: wh(15)]}, 2: {}}
                if has_prev:
                    p = b - 1
                    hooks[1].update({
                        (-1, 0): [lambda: stats_y(p, 0)],
                        (-1, 2): [lambda: ffn(p, 1), lambda: wh(11), lambda: stats_y(p, 1), lambda: wh(13), lambda: means_of(LN_Y, p), lambda: wh(15)],
                        (0, 3): [lambda: normalise_y(p, 0)], (1, 0): [lambda: normalise_y(p, 1)],
                    })
                if has_next:
                    s = b + 1
                    hooks[1].update({
                        (6, 0): [lambda: stats_x(s, 0)], (6, 3): [lambda: stats_x(s, half), lambda: means_of(LN_X, s)],
                        (7, 0): [lambda: normalise(LN_X, s, 0)], (7, 1): [lambda: normalise(LN_X, s, half)], (7, 3): [lambda: h0(s)],
                        (8, 0): [add_bias], (8, 2): [lambda: z_out(s, 0)], (9, 0): [lambda: z_out(s, 1)],
                    })
                    hooks[2].update({
                        (-1, 2): [lambda: x1(s, 0), lambda: stats_x1(s, 0), lambda: x1(s, 1)],
                        (0, 1): [lambda: stats_x1(s, half), lambda: means_of(LN_X1, s)], (0, 2): [lambda: normalise(LN_X1, s, 0)],
                        (0, 3): [lambda: normalise(LN_X1, s, half)], (1, 2): [lambda: h1(s, 0)], (2, 0): [lambda: h1(s, 1)],
                    })
                for layer in (1, 2):
                    def quad(g, l, full, u, layer=layer):
                        n = g * 4
                        s0 = 0 if layer == 1 else 4 * T

                        def masked_row(u=u):
                            if not live(layer, l, full, 5, u):
                                return
                            m, dq = (u + 5) % 4, (u + 5) // 4
                            if layer == 1 and m == 0:
                                dve.wait_ge(x_done, n + 8)
                                dve.sem_inc(held["dve"], 1)
                                nc.vector.tensor_copy(mask_row[:, :], mask_add[:, cols(l + 2, N, N)]).then_inc(row_done, 1)
                            hold(dve, "dve", bias_done, g + dq + 1)
                            hold(dve, "dve", z_done, n + u + 6)
                            if layer == 1:
                                if m == 0:
                                    if not full and l == -2:
                                        hold(dve, "dve", f2_ready, b * 2 * T + T)
                                    hold(dve, "dve", row_done, b * T + l + 3)
                                row, f2 = mask_row[:, :], cat[:, m, :]
                            else:
                                if m == 0 and l == -2:
                                    hold(dve, "dve", f2_ready, b * 2 * T + 2 * T)
                                tile = 4 * (l + dq) + m
                                row, f2 = mask_add[:, tile * N:(tile + 1) * N], f2o[:, :]
                            nc.vector.tensor_tensor_reduce(out=xr[:, m, :], in0=f2, in1=row, scale=1.0, scalar=MASKED * 2,
                                                           op0=ALU.add, op1=ALU.max, accum_out=mx[:, m:m + 1]).then_inc(x_done, 1)

                        def maxima():
                            f1 = (f1h if layer == 1 else f1o)[:, cols(l + 1, 4, 4)]
                            dve.wait_ge(x_done, n + 9)
                            nc.vector.scalar_tensor_tensor(zt[:, 0, :], mx[:, :], RATIO, f1, ALU.mult, ALU.add).then_inc(zt_done, 1)
                            dve.wait_ge(zt_done, g * 2 + 3)
                            nc.vector.scalar_tensor_tensor(zt[:, 1, :], zt[:, 0, :], 0.0, mx[:, :], ALU.max, ALU.add).then_inc(zt_done, 1)
                            dve.wait_ge(zt_done, g * 2 + 4)
                            nc.vector.tensor_scalar(shift[:, cols(l + 1, 4, 4, s0)], zt[:, 1, :], -UNIT, None, ALU.mult).then_inc(bias_done, 1)

                        post = layer == 1 and live(layer, l, full, -8)
                        if live(layer, l, full, -1, u):
                            k = (u - 1) % PAIR
                            dve.wait_ge(hi_done, n + u)
                            nc.vector.tensor_tensor(pt_lo[:, k, :], psum[k][:, :], pt_hi[:, k, :], ALU.subtract).then_inc(lo_done, 1)
                        if u == 0 and post:
                            dve.wait_ge(hthi_done, b * T + l - 1)
                            nc.vector.scalar_tensor_tensor(ht_lo, psD[:, :], scale(S_H), ht_hi, ALU.mult, ALU.subtract).then_inc(ht_done, 1)
                        late = not full and l == 0 and u in (0, 1)
                        if late and u == 1:
                            masked_row(0)
                        if not late or u == 1:
                            masked_row()
                        if live(layer, l, full, -2, u):
                            k = (u - 2) % 4
                            o = psC[:, (k % PAIR) * 512:(k % PAIR) * 512 + F + 1]
                            dve.wait_ge(mm_done, n + u - 1 + PAIR)
                            nc.vector.reciprocal(rden[:, k:k + 1], o[:, F:F + 1]).then_inc(rden_done, 1)
                            dve.wait_ge(rden_done, n + u - 1)
                            nc.vector.tensor_scalar(yq[:, k * F:(k + 1) * F], o[:, 0:F], rden[:, k:k + 1], scale(S_HINV if layer == 1 else S_OINV),
                                                    ALU.mult, ALU.mult).then_inc(y_done, 1)
                        if u == 2 and live(layer, l, full, 4):
                            maxima()
                        if u in (1, 2) and live(layer, l, full, -4):
                            part = slice((u - 1) * 2 * F, u * 2 * F)
                            dve.wait_ge(exp_done, g * 2 + u - 2)
                            nc.vector.tensor_scalar(eq[:, part], eq[:, part], 1.0, -1.0, ALU.min, ALU.add).then_inc(em1_done, 1)
                            dve.wait_ge(em1_done, g * 2 + u - 2)
                            to = (eq if layer == 1 else o2[l - 1])[:, part]
                            nc.vector.scalar_tensor_tensor(to, yq[:, part], 0.0, eq[:, part], ALU.max, ALU.add).then_inc(elu_done, 1)
                        if u == 1 and post:
                            dve.wait_ge(valohi_done, b * T + l - 1)
                            nc.vector.scalar_tensor_tensor(valo_lo[:, cols(l - 2, V, F)], psD[:, 0:F], VALO_SCALE, valo_hi[:, cols(l - 2, V, F)],
                                                           ALU.mult, ALU.subtract)
                            nc.vector.tensor_scalar(f1o[:, cols(l - 2, 1, 1)], psD[:, F:F + 1], scale(S_FO1), None, ALU.mult)
                            nc.vector.tensor_scalar(f2oc[:, :], psD[:, F + 1:F + 2], scale(S_FO2), None, ALU.mult).then_inc(f2c_done, 1)
                            dve.wait_ge(f2c_done, b * (T + 1) + l)
                            nc.vector.tensor_scalar(diag_o[:, :], ident[:, :], f2oc[:, :], None, ALU.mult).then_inc(diag_done, 1)
                    segment(dve, b, layer, quad, hooks[layer])

            dve.sem_inc(lo_done, PAIR)
            dve.sem_inc(y_done, PAIR)
            dve.sem_inc(bias_done, 1)
            dve.sem_inc(x_done, 1)
            batches(dve, body)
            dve.wait_ge(out_done, B * DMA)
            o2_out(B - 1, last_banks[1][0])
            for i, (bank, bank1) in enumerate(last_banks):
                ffn(B - 1, i, bank)
                stats_y(B - 1, i)
            means_of(LN_Y, B - 1)
            gain(B - 1, 0)
            gain(B - 1, 1)
            finish(B - 1, 0)
            finish(B - 1, 1)

        @block.tensor
        def _(pe):
            product, z, d, x1, h1 = tensor_stages(pe)

            def o2_T(p, k, bank=psD):
                pe.wait_ge(elu_done, (p * QB + QB) * 2)
                if k == 1 and bank is psD:
                    pe.wait_ge(o2t_act, p + 1)
                for t in range(T):
                    last = nc.tensor.transpose(bank[:, t * P:(t + 1) * P], o2t[t // 4][:, t % 4, k * P:(k + 1) * P], ident[:, :])
                last.then_inc(o2t_ps, 1)

            def ff1(p, m, bank=psD):
                pe.wait_ge(o2t_act, p + 1)
                pe.wait_ge(o2t_dve, p + 1)
                if m == 1 and bank is psD:
                    pe.wait_ge(ff1_done, p * 2 + 1)
                for c in range(2):
                    last = product(bank[:, c * 512:(c + 1) * 512],
                                   [(w1_sb[:, k, m * P:(m + 1) * P], o2T[:, k, c * 512:(c + 1) * 512]) for k in range(KF)])
                last.then_inc(ff1_ps, 1)

            def ff2(p, i, bank=psD):
                pe.wait_ge(ff1_done, p * 2 + 2)
                if i == 1 and bank is psD:
                    pe.wait_ge(ffn_done, p * 2 + 1)
                for t in range(T // 2):
                    tok = slice((i * 4 + t) * P, (i * 4 + t + 1) * P)
                    last = product(bank[:, t * F:(t + 1) * F], [(ffT[k][:, tok], w2_sb[:, k, :]) for k in range(KF)])
                last.then_inc(ff2_ps, 1)

            def body(b, has_prev, has_next):
                pe.wait_ge(h1_done, b * 2 + 2)
                three = [(h1_hi, wh_hi), (h1_hi, wh_lo), (h1_lo, wh_hi)]
                for jt in range(T):
                    tok = slice(jt * P, (jt + 1) * P)
                    last = product(psD[:, jt * NF:(jt + 1) * NF], [(h[:, k, tok], w[:, k, HF:HF + NF]) for k in range(KF) for h, w in three])
                last.then_inc(f_ps, 1)

                def wh(i):
                    jt, c = i // 2, i % 2
                    tok = slice(jt * P, (jt + 1) * P)
                    if 2 <= jt < T - 1 and c == 0:
                        pe.wait_ge(wh_done, b * T + jt - 1)
                    if jt == T - 1 and c == 0:
                        pe.wait_ge(f2_ready, b * 2 * T + T)
                    last = product(wh_bank[jt][:, c * 512:(c + 1) * 512],
                                   [(h[:, k, tok], w[:, k, c * 512:(c + 1) * 512]) for k in range(KF) for h, w in three])
                    if c:
                        last.then_inc(wh_ps, 1)

                def row(jt):
                    if jt == 0:
                        pe.wait_ge(y_done, b * UB + PAIR)
                    pe.wait_ge(diag_done, b * 2 * T + jt + 1)
                    if jt >= 2:
                        pe.wait_ge(f2_ready, b * 2 * T + jt - 1)
                    pe.wait_ge(diaglo_done, b * T + jt + 1)
                    product(psC[:, jt % 2 * 512:(jt % 2 + 1) * 512], [(ones16[:, :], diag[:, part, :]) for part in (0, 1)]).then_inc(bc_ps, 1)

                p = b - 1
                wh_steps(wh, row, {
                    1: [lambda: pe.wait_ge(f2c_done, b * (T + 1) + 1), lambda: o2_T(p, 0)],
                    3: [lambda: o2_T(p, 1)], 4: [lambda: ff1(p, 0)], 5: [lambda: ff1(p, 1)], 6: [lambda: ff2(p, 0)], 9: [lambda: ff2(p, 1)],
                } if has_prev else {})
                hooks = {1: {}, 2: {}}
                if has_next:
                    s = b + 1
                    hooks[1].update({
                        (8, 0): [lambda: z(s, 0, 0)], (8, 1): [lambda: z(s, 0, 1), lambda: d(s, 0)],
                        (8, 2): [lambda: pe.wait_ge(y_done, b * UB + 4 * T + PAIR), lambda: z(s, 1, 0)],
                        (8, 3): [lambda: z(s, 1, 1), lambda: d(s, 1)],
                        (9, 1): [lambda: x1(s, 0, 0, 2)],
                        (9, 3): [lambda: x1(s, 0, 2, 2), lambda: x1(s, 1, 0, 4)],
                    })
                    hooks[2].update({
                        (-1, 3): [lambda: pe.wait_ge(x1_done, s * 3 + 2)], (0, 0): [lambda: pe.wait_ge(x1_done, s * 3 + 3)],
                        (1, 0): [lambda: h1(s, 0)], (1, 2): [lambda: h1(s, 1)],
                    })
                for layer in (1, 2):
                    def quad(g, l, full, u, layer=layer):
                        n = g * 4
                        if live(layer, l, full, 0, u):
                            pe.wait_ge(p_done, n + u + 1 + PAIR)
                            pe.wait_ge(lo_done, n + u + 1)
                            if layer == 1 and not full and l == 0 and u < PAIR:
                                pe.wait_ge(wh_done, b * T + T - 1)
                            for t in range(T):
                                last = nc.tensor.transpose(psum[u % PAIR][:, t * P:(t + 1) * P], pr[:, u % PAIR, t * P:(t + 1) * P], ident[:, :])
                            last.then_inc(pt_ps, 1)
                        if live(layer, l, full, -1, u):
                            m = (u - 1) % 4
                            o = psC[:, (m % PAIR) * 512:(m % PAIR) * 512 + 512]
                            hi, lo = pt_hi[:, m % PAIR, :], pt_lo[:, m % PAIR, :]
                            pe.wait_ge(y_done, n + u)
                            if layer == 1 and not full and l == 0 and u == 1:
                                pe.wait_ge(wh_done, b * T + T)
                            pe.wait_ge(hi_done, n + u)
                            for t in range(T):
                                vh = val_hi[:, t, m, 0:F + 1] if layer == 1 else valo_hi[:, t * V:t * V + F + 1]
                                vl = val_lo[:, t, m, 0:F] if layer == 1 else valo_lo[:, t * V:t * V + F]
                                nc.tensor.matmul(o[:, 0:F + 1], hi[:, t * P:(t + 1) * P], vh, start=t == 0, stop=False)
                                nc.tensor.matmul(o[:, 0:F], hi[:, t * P:(t + 1) * P], vl, start=False, stop=False)
                            pe.wait_ge(lo_done, n + u + PAIR)
                            for t in range(T):
                                vh = val_hi[:, t, m, 0:F + 1] if layer == 1 else valo_hi[:, t * V:t * V + F + 1]
                                last = nc.tensor.matmul(o[:, 0:F + 1], lo[:, t * P:(t + 1) * P], vh, start=False, stop=t == T - 1)
                            last.then_inc(mm_done, 1)
                        if u == 2 and layer == 1 and live(layer, l, full, -8):
                            pe.wait_ge(diag_done, b * 2 * T + T + l - 1)
                            nc.tensor.matmul(psD[:, 512:512 + P], ones[:, :], diag_o[:, :], start=True, stop=True).then_inc(bc_ps, 1)
                        if u == 0 and layer == 1 and live(layer, l, full, -8):
                            pe.wait_ge(ht_done, b * T + l - 1)
                            product(psD[:, 0:V], [(h[:, k * P:(k + 1) * P], w[:, k, :]) for k in range(KH)
                                                  for h, w in ((ht_hi, wo_hi), (ht_hi, wo_lo), (ht_lo, wo_hi))]).then_inc(proj_ps, 1)
                        if u == 3 and layer == 1 and live(layer, l, full, -4):
                            pe.wait_ge(elu_done, g * 2)
                            pe.wait_ge(f2_ready, b * 2 * T + T + l - 1)
                            for k in range(KH):
                                last = nc.tensor.transpose(psD[:, k * P:(k + 1) * P], eq[:, k * P:(k + 1) * P], ident[:, :])
                            last.then_inc(ht_ps, 1)
                    segment(pe, b, layer, quad, hooks[layer])

            pe.sem_inc(mm_done, PAIR)
            pe.sem_inc(ht_ps, 1)
            pe.sem_inc(proj_ps, 1)
            batches(pe, body)
            for i, (bank, bank1) in enumerate(last_banks):
                o2_T(B - 1, i, bank)
            for i, (bank, bank1) in enumerate(last_banks):
                ff1(B - 1, i, bank1)
            for i, (bank, bank1) in enumerate(last_banks):
                ff2(B - 1, i, bank)


_INS = ['x', 'adj', 'L0_gnn_W', 'L0_gnn_b', 'L1_gnn_W_heads', 'L1_gnn_a_heads', 'L1_gnn_W_out', 'L1_gnn_a_out',
        'L1_gnn_w1', 'L1_gnn_b1', 'L1_gnn_w2', 'L1_gnn_b2', 'L1_gnn_ln_gamma', 'L1_gnn_ln_beta']


def kernel(**inputs):
    import numpy as np
    import concourse.bacc as bacc
    from concourse.bass_utils import run_bass_kernel_spmd

    nc = bacc.Bacc("TRN2", target_bir_lowering=False, num_devices=1)
    arrays, args = {}, []
    for name in _INS:
        a = np.ascontiguousarray(inputs[name])
        arrays[f"in_{name}"] = a
        args.append(nc.dram_tensor(f"in_{name}", a.shape, mybir.dt.from_np(a.dtype), kind="ExternalInput").ap())
    out = nc.dram_tensor("out", arrays["in_x"].shape, F32, kind="ExternalOutput").ap()
    build(nc, *args, out)
    r = run_bass_kernel_spmd(nc, [arrays], core_ids=[0])
    return r.results[0]["out"]
```
